# Optimizing a Trainium2 kernel written in Bass

```python
import numpy as np
import jax
import jax.numpy as jnp

def _softmax(x, axis=-1):
    return jax.nn.softmax(x, axis=axis)

def _gelu(x):
    return jax.nn.gelu(x, approximate=True)

def _silu(x):
    return jax.nn.silu(x)

def _sigmoid(x):
    return jax.nn.sigmoid(x)

def _layernorm(x, axis=-1, eps=1e-05):
    m = jnp.mean(x, axis=axis, keepdims=True)
    v = jnp.var(x, axis=axis, keepdims=True)
    return (x - m) / jnp.sqrt(v + eps)

def _scatter_add(tgt, idx, src, axis=0):
    return tgt.at[idx].add(src)

def _segment_sum(src, seg, n):
    return jax.ops.segment_sum(src, seg, n)
kernel_name = 'mk_macaron_d1_jaxref_r8_5af665'

def setup_inputs(seed: int=0):
    np.random.seed(seed)
    _w = jnp.asarray

    def _L0_attn_setup():
        import jax, jax.numpy as jnp
        import numpy as np
        EMBED_DIM = 128
        NUM_HEADS = 16
        HEAD_DIM = EMBED_DIM // NUM_HEADS

        def _sinusoid_pos_emb(seq_len, dim):
            pos = jnp.arange(seq_len, dtype=jnp.float32)
            idx = jnp.arange(dim // 2, dtype=jnp.float32)
            inv_freq = 1.0 / 10000.0 ** (2.0 * idx / dim)
            ang = pos[:, None] * inv_freq[None, :]
            return jnp.concatenate([jnp.sin(ang), jnp.cos(ang)], axis=-1)

        def _relative_shift(x):
            b, h, s, _ = x.shape
            x = jnp.pad(x, ((0, 0), (0, 0), (0, 0), (1, 0)))
            x = x.reshape(b, h, s + 1, s)
            return x[:, :, 1:, :].reshape(b, h, s, s)
        key = jax.random.key(seed)
        ks = jax.random.split(key, 12)
        D = EMBED_DIM
        sc = 1.0 / np.sqrt(D)
        inp = {'x': jax.random.normal(ks[0], (2, 256, D), dtype=jnp.float32)}
        for i, name in enumerate(['Wq', 'Wk', 'Wv', 'Wp', 'Wo']):
            inp[name] = jax.random.normal(ks[1 + i], (D, D), dtype=jnp.float32) * sc
            inp['b' + name[1].lower()] = jnp.zeros((D,), dtype=jnp.float32)
        inp['u'] = jax.random.normal(ks[6], (1, NUM_HEADS, 1, HEAD_DIM), dtype=jnp.float32) * 0.05
        inp['v'] = jax.random.normal(ks[7], (1, NUM_HEADS, 1, HEAD_DIM), dtype=jnp.float32) * 0.05
        return inp
    _L0_attn_in = _L0_attn_setup()

    def _L0_ffn_setup():
        import jax, jax.numpy as jnp
        import numpy as np
        LN_EPS = 1e-05

        def layer_norm(x, g, b):
            mu = jnp.mean(x, axis=-1, keepdims=True)
            var = jnp.mean(jnp.square(x - mu), axis=-1, keepdims=True)
            return (x - mu) * jax.lax.rsqrt(var + LN_EPS) * g + b

        def ternary_quant(w):
            scale = 1.0 / jnp.clip(jnp.mean(jnp.abs(w)), 1e-05)
            wq = jnp.clip(jnp.round(w * scale), -1.0, 1.0) / scale
            return w + jax.lax.stop_gradient(wq - w)
        key = jax.random.key(seed)
        ks = jax.random.split(key, 3)
        dim, hidden = (128, 512)
        B, S = (8, 128)
        x = jax.random.normal(ks[0], (B, S, dim), dtype=jnp.float32)
        w1 = jax.random.normal(ks[1], (hidden, dim), dtype=jnp.float32) * 0.02
        w2 = jax.random.normal(ks[2], (dim, hidden), dtype=jnp.float32) * 0.02
        return {'x': x, 'ln1_g': jnp.ones((dim,), jnp.float32), 'ln1_b': jnp.zeros((dim,), jnp.float32), 'w1': w1, 'b1': jnp.zeros((hidden,), jnp.float32), 'ln2_g': jnp.ones((hidden,), jnp.float32), 'ln2_b': jnp.zeros((hidden,), jnp.float32), 'w2': w2, 'b2': jnp.zeros((dim,), jnp.float32)}
    _L0_ffn_in = _L0_ffn_setup()
    _d = {'L0_attn_x': _L0_attn_in['x'], 'L0_attn_Wq': _L0_attn_in['Wq'], 'L0_attn_bq': _L0_attn_in['bq'], 'L0_attn_Wk': _L0_attn_in['Wk'], 'L0_attn_bk': _L0_attn_in['bk'], 'L0_attn_Wv': _L0_attn_in['Wv'], 'L0_attn_bv': _L0_attn_in['bv'], 'L0_attn_Wp': _L0_attn_in['Wp'], 'L0_attn_bp': _L0_attn_in['bp'], 'L0_attn_Wo': _L0_attn_in['Wo'], 'L0_attn_bo': _L0_attn_in['bo'], 'L0_attn_u': _L0_attn_in['u'], 'L0_attn_v': _L0_attn_in['v'], 'L0_ffn_ln1_g': _L0_ffn_in['ln1_g'], 'L0_ffn_ln1_b': _L0_ffn_in['ln1_b'], 'L0_ffn_w1': _L0_ffn_in['w1'], 'L0_ffn_b1': _L0_ffn_in['b1'], 'L0_ffn_ln2_g': _L0_ffn_in['ln2_g'], 'L0_ffn_ln2_b': _L0_ffn_in['ln2_b'], 'L0_ffn_w2': _L0_ffn_in['w2'], 'L0_ffn_b2': _L0_ffn_in['b2']}
    _x0 = _d['L0_attn_x']
    _d['L0_attn_x'] = jax.random.normal(jax.random.fold_in(jax.random.key(seed), 1), (4, 512, 128), dtype=_x0.dtype)
    del _x0
    return _d

def reference(L0_attn_x, L0_attn_Wq, L0_attn_bq, L0_attn_Wk, L0_attn_bk, L0_attn_Wv, L0_attn_bv, L0_attn_Wp, L0_attn_bp, L0_attn_Wo, L0_attn_bo, L0_attn_u, L0_attn_v, L0_ffn_ln1_g, L0_ffn_ln1_b, L0_ffn_w1, L0_ffn_b1, L0_ffn_ln2_g, L0_ffn_ln2_b, L0_ffn_w2, L0_ffn_b2):

    def _L0_attn_ref(x, Wq, bq, Wk, bk, Wv, bv, Wp, bp, Wo, bo, u, v):
        import jax, jax.numpy as jnp
        import numpy as np
        EMBED_DIM = 128
        NUM_HEADS = 16
        HEAD_DIM = EMBED_DIM // NUM_HEADS

        def _sinusoid_pos_emb(seq_len, dim):
            pos = jnp.arange(seq_len, dtype=jnp.float32)
            idx = jnp.arange(dim // 2, dtype=jnp.float32)
            inv_freq = 1.0 / 10000.0 ** (2.0 * idx / dim)
            ang = pos[:, None] * inv_freq[None, :]
            return jnp.concatenate([jnp.sin(ang), jnp.cos(ang)], axis=-1)

        def _relative_shift(x):
            b, h, s, _ = x.shape
            x = jnp.pad(x, ((0, 0), (0, 0), (0, 0), (1, 0)))
            x = x.reshape(b, h, s + 1, s)
            return x[:, :, 1:, :].reshape(b, h, s, s)
        B, S, D = x.shape
        H, P = (NUM_HEADS, HEAD_DIM)

        def heads(t):
            return t.reshape(B, S, H, P).transpose(0, 2, 1, 3)
        q = heads(x @ Wq + bq)
        k = heads(x @ Wk + bk)
        val = heads(x @ Wv + bv)
        pos = _sinusoid_pos_emb(S, D) @ Wp + bp
        pos = pos.reshape(S, H, P).transpose(1, 0, 2)
        content_score = jnp.einsum('bhsp,bhtp->bhst', q + u, k)
        pos_score = jnp.einsum('bhsp,htp->bhst', q + v, pos)
        pos_score = _relative_shift(pos_score)
        score = (content_score + pos_score) / jnp.sqrt(jnp.float32(P))
        weights = jax.nn.softmax(score, axis=-1)
        out = jnp.einsum('bhst,bhtp->bhsp', weights, val)
        out = out.transpose(0, 2, 1, 3).reshape(B, S, D)
        return out @ Wo + bo

    def _L0_ffn_ref(x, ln1_g, ln1_b, w1, b1, ln2_g, ln2_b, w2, b2):
        import jax, jax.numpy as jnp
        import numpy as np
        LN_EPS = 1e-05

        def layer_norm(x, g, b):
            mu = jnp.mean(x, axis=-1, keepdims=True)
            var = jnp.mean(jnp.square(x - mu), axis=-1, keepdims=True)
            return (x - mu) * jax.lax.rsqrt(var + LN_EPS) * g + b

        def ternary_quant(w):
            scale = 1.0 / jnp.clip(jnp.mean(jnp.abs(w)), 1e-05)
            wq = jnp.clip(jnp.round(w * scale), -1.0, 1.0) / scale
            return w + jax.lax.stop_gradient(wq - w)
        h = layer_norm(x, ln1_g, ln1_b)
        h = jnp.einsum('bsd,hd->bsh', h, ternary_quant(w1)) + b1
        h = jax.nn.gelu(h, approximate=False)
        h = layer_norm(h, ln2_g, ln2_b)
        out = jnp.einsum('bsh,dh->bsd', h, ternary_quant(w2)) + b2
        return out
    x = L0_attn_x
    x = x + 0.5 * _L0_ffn_ref(_layernorm(x, axis=-1), L0_ffn_ln1_g, L0_ffn_ln1_b, L0_ffn_w1, L0_ffn_b1, L0_ffn_ln2_g, L0_ffn_ln2_b, L0_ffn_w2, L0_ffn_b2)
    x = x + _L0_attn_ref(_layernorm(x, axis=-1), L0_attn_Wq, L0_attn_bq, L0_attn_Wk, L0_attn_bk, L0_attn_Wv, L0_attn_bv, L0_attn_Wp, L0_attn_bp, L0_attn_Wo, L0_attn_bo, L0_attn_u, L0_attn_v)
    x = x + 0.5 * _L0_ffn_ref(_layernorm(x, axis=-1), L0_ffn_ln1_g, L0_ffn_ln1_b, L0_ffn_w1, L0_ffn_b1, L0_ffn_ln2_g, L0_ffn_ln2_b, L0_ffn_w2, L0_ffn_b2)
    return x

_drawn_inputs = setup_inputs


def setup_inputs(seed=0):
    import zlib

    import numpy as np

    out = dict(_drawn_inputs(seed))
    spreads = {'L0_attn_bq': (0.0, 0.717),
     'L0_attn_bk': (0.0, 0.8),
     'L0_attn_bv': (0.0, 0.1),
     'L0_attn_bp': (0.0, 0.8),
     'L0_attn_bo': (0.0, 0.1),
     'L0_ffn_ln1_g': (1.0, 0.2),
     'L0_ffn_ln1_b': (0.0, 0.275),
     'L0_ffn_b1': (0.0, 0.1),
     'L0_ffn_ln2_g': (1.0, 0.2),
     'L0_ffn_ln2_b': (0.0, 0.284),
     'L0_ffn_b2': (0.0, 0.1)}
    factors = {'L0_attn_u': 8.0, 'L0_attn_v': 8.0}
    for name, (base, spread) in spreads.items():
        noise = np.random.default_rng([zlib.crc32(name.encode()), seed]).standard_normal(out[name].shape)
        drawn = base * np.exp(spread * noise) if base else spread * noise
        out[name] = jnp.asarray(drawn.astype(out[name].dtype))
    for name, factor in factors.items():
        out[name] = (out[name] * factor).astype(out[name].dtype)
    return out
```

```python
from contextlib import ExitStack

import numpy as np

import concourse.bass as bass
from concourse import mybir

F32 = mybir.dt.float32
F16 = mybir.dt.float16
U32 = mybir.dt.uint32
ALU = mybir.AluOpType
ACT = mybir.ActivationFunctionType
AX = mybir.AxisListType

B, S, D = 4, 512, 128
H, HP = 16, 8
HID = 512
NT = B * S // 128
HC = HID // 128
NI = 8
NQ = S // 4 // NI
NG = S // NI
KB = S // 32
EPS = 1e-5
SCALE = float(HP) ** -0.5
SB = 4
ZW = 2 * S - NI
ZB0 = S - NI + 2
LOADS = 16


def macaron_kernel(nc, ins, out):
    (x_d, wq_d, bq_d, wk_d, bk_d, wv_d, bv_d, wp_d, bp_d, wo_d, bo_d, u_d, v_d,
     g1_d, lb1_d, w1_d, b1_d, g2_d, lb2_d, w2_d, b2_d, embT_d, ident_d) = ins

    qs_dram = nc.dram_tensor("qs_scratch", (D, 2, 3, B * S), F16, kind="Internal").ap()
    qc_dram = nc.dram_tensor("qc_scratch", (D, 4, B * S), F16, kind="Internal").ap()
    kc_dram = nc.dram_tensor("kc_scratch", (D, 4, B, S), F16, kind="Internal").ap()
    z_dram = nc.dram_tensor("z_scratch", (D, 2, 3, 2 * S), F16, kind="Internal").ap()
    at_dram = nc.dram_tensor("attn_scratch", (H, HP, 16, 128), F32, kind="Internal").ap()

    with ExitStack() as ctx:
        def sb(name, shape, dt=F32):
            return ctx.enter_context(nc.sbuf_tensor(name, shape, dt))

        def sem(name):
            return ctx.enter_context(nc.semaphore(name))

        x = sb("x", [128, NT, D])
        xT = sb("xT", [128, B * S])
        xh = sb("xh", [128, 4, D])
        ident = sb("ident", [128, 128])
        ones = sb("ones", [128, 128])
        w1T = sb("w1T", [128, HID])
        w2T = sb("w2T", [128, HC, D])
        w2g = sb("w2g", [128, HC, D])
        b1row = sb("b1row", [128, HID])
        half_const = sb("half_const", [128, D])
        bo_row = sb("bo_row", [128, D])
        wo_sb = sb("wo_sb", [128, D])
        cols = sb("cols", [128, 32])
        minus_half = sb("minus_half", [128, 4])
        stat = sb("stat", [128, 2, 6])
        mv = sb("mv", [128, NT, 2])
        rs = sb("rs", [128, NT])
        gstat = sb("gstat", [128, 2, 6])
        gmv = sb("gmv", [128, NT, 2])
        grs = sb("grs", [128, NT])
        stage_q = sb("stage_q", [128, 2, 3, B * S], F16)
        stage_c = sb("stage_c", [128, 2, B * S], F16)
        stage_k = sb("stage_k", [128, 2, S], F16)
        stage_z = sb("stage_z", [128, 2, 3, ZW], F16)
        probs = sb("probs", [128, 4, S])
        negmax = sb("negmax", [128, 8])
        rowsum = sb("rowsum", [128, H * NQ])
        pT = sb("pT", [128, 2, NQ, S])
        v_rep = sb("v_rep", [128, B * KB, D])
        v_diag = sb("v_diag", [128, 2, B * KB, 4, HP])
        o_sb = sb("o_sb", [128, 2, 128])
        ps = [ctx.enter_context(nc.psum_tensor(f"ps{i}", [128, 512], F32)) for i in range(8)]

        pTf = pT[:, :, :, :].rearrange("p a q s -> p (a q s)")
        wq_sb, wk_sb, wv_sb, wp_sb = (pTf[:, 128 * n:128 * n + 128] for n in range(4))
        embT = pTf[:, 512:1024]
        bv_row = pTf[:, 1024:1152]
        qf = pTf[:, 2048:3072].rearrange("p (a n) -> p a n", a=2)
        kf = pTf[:, 3072:3584]
        pf = pTf[:, 3584:4096]
        half = pTf[:, 4096:4096 + 6 * 1024].bitcast(F16).rearrange("p (a n) -> p a n", a=6)
        uh, ul, vh, vl, kh, kl = (half[:, n, :] for n in range(6))
        zs = pTf[:, 10240:12288].bitcast(F16).rearrange("p (a n) -> p a n", a=4)
        v_sb = pTf[:, 12288:14336].rearrange("p (t n) -> p t n", t=NT)
        w1_sb = pTf[:, 14336:14848].rearrange("p (c n) -> p c n", c=HC)
        w2_sb = pTf[:, 14848:15360]
        tern = pTf[:, 15360:16384].rearrange("p (a n) -> p a n", a=2)
        tmp_t = pTf[:, 4096:5120].rearrange("p (a n) -> p a n", a=2)
        lb2_rep = pTf[:, 5120:5632].rearrange("p (c n) -> p c n", c=HC)
        b2_row = pTf[:, 5632:5760]
        vrf = v_rep[:, :, :].rearrange("p a n -> p (a n)")
        hs = vrf[:, 0:1024].rearrange("p (a n) -> p a n", a=2)
        ge = vrf[:, 1024:2560].rearrange("p (a n) -> p a n", a=3)
        gn = vrf[:, 2560:3584].rearrange("p (a n) -> p a n", a=2)
        gT = vrf[:, 3584:4608].rearrange("p (a n) -> p a n", a=2)
        attnT = pTf[:, 0:2048]
        rec = pTf[:, 2048:2304]
        recx = pTf[:, 4096:6144].rearrange("p (q h e) -> p q h e", q=NQ, h=H)

        g1c, lb1c, bqc, uc, vc, bkc, bpc = (cols[:, n:n + 1] for n in range(7))
        quc, qvc = cols[:, 7:8], cols[:, 8:9]
        g2c, lb2c = cols[:, 9:13], cols[:, 13:17]
        wsum, wclip, wscale, wstep = (cols[:, n:n + 2] for n in (17, 19, 21, 23))

        x_in = sem("x_in")
        weights_in = sem("weights_in")
        qkv_weights_in = sem("qkv_weights_in")
        ones_set = sem("ones_set")
        wsum_ready = sem("wsum_ready")
        wtotal_ready = sem("wtotal_ready")
        dve_step = sem("dve_step")
        tern_ready = sem("tern_ready")
        tern_turned = sem("tern_turned")
        w1_ready = sem("w1_ready")
        w2_ready = sem("w2_ready")
        lb2_ready = sem("lb2_ready")
        const_summed = sem("const_summed")
        const_ready = sem("const_ready")
        bias_cols_ready = sem("bias_cols_ready")
        stage_zero = sem("stage_zero")
        ln = [{n: sem(f"{n}{f}") for n in ("stat", "mean", "rstd0_", "rstd", "xhat", "turned", "xT")}
              for f in range(3)]
        ff = [{n: sem(f"{n}{f}") for n in ("hid", "hid_biased", "gelu", "gstat", "gmean", "gvar", "grstd",
                                          "gnorm", "gturned", "gT", "ffn", "x_const", "x_new")}
              for f in range(2)]
        pos_mm = sem("pos_mm")
        pos_f = sem("pos_f")
        pos_split = sem("pos_split")
        zs_zero = sem("zs_zero")
        q_mm = sem("q_mm")
        k_mm = sem("k_mm")
        v_mm = sem("v_mm")
        q_f = sem("q_f")
        k_f = sem("k_f")
        q_high = sem("q_high")
        q_split = sem("q_split")
        k_high = sem("k_high")
        k_split = sem("k_split")
        v_ready = sem("v_ready")
        v_rep_in = sem("v_rep_in")
        scratch_out = sem("scratch_out")
        staged = [sem("staged_even"), sem("staged_odd")]
        v_diag_ready = sem("v_diag_ready")
        v_diag_zero = sem("v_diag_zero")
        scores_ready = sem("scores_ready")
        max_ready = sem("max_ready")
        probs_ready = sem("probs_ready")
        pT_ready = sem("pT_ready")
        av_ready = sem("av_ready")
        o_ready = sem("o_ready")
        o_out = [sem("o_out_even"), sem("o_out_odd")]
        attn_in = sem("attn_in")
        rec_ready = sem("rec_ready")
        recx_ready = sem("recx_ready")
        rec_turned = sem("rec_turned")
        attn_scaled = sem("attn_scaled")
        wo_mm = sem("wo_mm")
        x_bo = sem("x_bo")
        x_attn = sem("x_attn")
        out_done = sem("out_done")

        x_of = [x_in, ff[0]["x_new"], x_attn]

        def x_made(eng, f, t):
            eng.wait_ge(x_of[f], 16 * B if f == 0 else t + 1)

        block = ctx.enter_context(nc.Block())

        def row(ap, n):
            return bass.AP(ap.tensor, ap.offset, [[0, 128], [1, n]])

        def col(ap):
            return ap.rearrange("(p a) -> p a", a=1)

        @block.sync
        def _(sp):
            xv = x_d.rearrange("b (t p) d -> b p t d", p=128)
            for b in range(B):
                sp.dma_start(x[:, 4 * b:4 * b + 4, :], xv[b]).then_inc(x_in, 16)
            sp.wait_ge(pos_split, 2)
            for t, kind, src in ((0, 0, 0), (1, 0, 2), (0, 1, 0), (1, 1, 1), (0, 2, 2), (1, 2, 3)):
                sp.dma_start(z_dram[:, t, kind, :], zs[:, src, :]).then_inc(scratch_out, 16)
            for b in range(B):
                c = slice(b * S, (b + 1) * S)
                sp.wait_ge(q_split, b + 1)
                for t, src in ((0, uh), (1, uh), (2, ul), (3, ul)):
                    sp.dma_start(qc_dram[:, t, c], src[:, c]).then_inc(scratch_out, 16)
                for t, kind, src in ((0, 0, vl), (0, 1, vh), (1, 1, vh)):
                    sp.dma_start(qs_dram[:, t, kind, c], src[:, c]).then_inc(scratch_out, 16)
                n = (NI - 1) * NG
                for t, kind, src in ((1, 0, vl), (0, 2, vh), (1, 2, vh)):
                    sp.dma_start(qs_dram[:, t, kind, b * S:b * S + n],
                                 src[:, b * S + NG:(b + 1) * S]).then_inc(scratch_out, 16)
                    sp.dma_start(qs_dram[:, t, kind, b * S + n:(b + 1) * S],
                                 src[:, b * S + 1:b * S + 1 + NG]).then_inc(scratch_out, 16)
                sp.wait_ge(k_split, b + 1)
                for t, src in ((0, kh), (1, kl), (2, kh), (3, kl)):
                    sp.dma_start(kc_dram[:, t, b, :], src[:, c]).then_inc(scratch_out, 16)
            sp.wait_ge(ff[0]["x_new"], NT)
            sp.wait_ge(v_ready, NT)
            vr = v_rep[:, :, :].rearrange("p (t k) n -> p t k n", k=4)
            for quad in range(4):
                for kq in range(4):
                    sp.dma_start(vr[32 * quad:32 * quad + 32, :, kq, :],
                                 v_sb[32 * kq:32 * kq + 32, :, :]).then_inc(v_rep_in, 16)
            n_scratch = 6 + B * (4 + 3 + 6 + 4)
            sp.wait_ge(scratch_out, 16 * n_scratch)
            sp.wait_ge(stage_zero, 4)

            def stage(h, par):
                q_rows = qs_dram.rearrange("(h p) t k n -> h (p t) k n", p=HP)[h]
                c_rows = qc_dram.rearrange("(h p) t n -> h (p t) n", p=HP)[h]
                k_rows = kc_dram.rearrange("(h p) t b n -> h b (p t) n", p=HP)[h]
                z_rows = z_dram.rearrange("(h p) t k n -> h (p t) k n", p=HP)[h]
                done = staged[par]
                for ii in range(NI):
                    i = NI - 1 - ii
                    src = q_rows.rearrange("r k (b m) -> r (k b) m", b=B)[:, :, i * NG:(i + 1) * NG]
                    dst = stage_q[16 * ii:16 * ii + 16, par, :, :].rearrange(
                        "r k (b m) -> r (k b) m", b=B)[:, :, i * NG:(i + 1) * NG]
                    sp.dma_start(dst, src).then_inc(done, 16)
                for b in range(B):
                    sp.dma_start(stage_c[32 * b:32 * b + 32, par, b * S:(b + 1) * S],
                                 c_rows[:, b * S:(b + 1) * S]).then_inc(done, 16)
                sp.dma_start(stage_k[:, par, :], k_rows).then_inc(done, 16)
                for kind, lo, hi in ((0, 0, ZW), (1, 0, S), (2, ZB0, ZW)):
                    zr = z_rows[:, kind, :]
                    src = bass.AP(zr.tensor, zr.offset + lo, [[1, NI]] + [list(zr.ap[0])] + [[1, hi - lo]])
                    sp.dma_start(stage_z[:, par, kind, lo:hi], src).then_inc(done, 16)

            stage(0, 0)
            stage(1, 1)
            sp.wait_ge(scores_ready, NQ)
            stage(2, 0)

            def send_o(h, par):
                sp.wait_ge(o_ready, h + 1)
                sp.dma_start(at_dram[h].rearrange("p j n -> j p n"),
                             o_sb[:, par, :]).then_inc(o_out[par], 16)

            with sp.Fori(0, (H - 4) // 2) as it:
                for k in range(2):
                    par = (3 + k) % 2
                    sp.wait_ge(scores_ready, (it * 2 + (2 + k)) * NQ)
                    stage(it * 2 + (3 + k), par)
                    send_o(it * 2 + k, k)
            sp.wait_ge(scores_ready, (H - 2) * NQ)
            stage(H - 1, 1)
            for h in range(H - 4, H):
                send_o(h, h % 2)
            for par in range(2):
                sp.wait_ge(o_out[par], 16 * (H // 2))
            sp.dma_start(attnT, at_dram.rearrange("h p j n -> (h p) (j n)")).then_inc(attn_in, 16)
            ov = out.rearrange("b (t p) d -> (b t) p d", p=128)
            for t in range(NT):
                sp.wait_ge(ff[1]["x_new"], t + 1)
                sp.dma_start(ov[t], x[:, t, :]).then_inc(out_done, 16)
            sp.wait_ge(out_done, 16 * NT)

        @block.gpsimd
        def _(pool):
            nc.gpsimd.memset(ones[:, :], 1.0).then_inc(ones_set, 1)
            nc.gpsimd.memset(minus_half[:, :], -0.5).then_inc(ones_set, 1)
            pool.wait_ge(ones_set, 2)
            nc.gpsimd.memset(zs[:, :, :], 0.0).then_inc(zs_zero, 1)

            def ln_rstd(f):
                s = ln[f]
                for g in range(B):
                    var, r = mv[:, 4 * g:4 * g + 4, 1], rs[:, 4 * g:4 * g + 4]
                    pool.wait_ge(s["mean"], 4 * g + 4)
                    m, a = (1.0, EPS) if f == 1 else (1 + EPS, EPS * EPS)
                    nc.gpsimd.tensor_scalar(r, var, m, a, ALU.mult, ALU.add).then_inc(s["rstd0_"], 1)
                    pool.wait_ge(s["rstd0_"], g + 1)
                    nc.gpsimd.tensor_tensor(r, r, minus_half[:, :], ALU.pow).then_inc(s["rstd"], 1)

            def ffn_small(f):
                s = ff[f]
                for t in range(NT):
                    if t % 4 == 0:
                        pool.wait_ge(ln[2 * f]["xhat"], t + 4)
                    if t == 0 and f == 0:
                        pool.wait_ge(const_ready, 1)
                    nc.gpsimd.tensor_tensor(x[:, t, :], x[:, t, :], half_const[:, :], ALU.add)\
                        .then_inc(s["x_const"], 1)
                    pool.wait_ge(s["gmean"], t + 1)
                    r = grs[:, t:t + 1]
                    nc.gpsimd.tensor_scalar(r, gmv[:, t, 1:2], 1.0, EPS, ALU.mult, ALU.add)\
                        .then_inc(s["gvar"], 1)
                    pool.wait_ge(s["gvar"], t + 1)
                    nc.gpsimd.tensor_tensor(r, r, minus_half[:, 0:1], ALU.pow).then_inc(s["grstd"], 1)

            ln_rstd(0)
            for par in range(2):
                nc.gpsimd.memset(stage_q[:, par, :, :].bitcast(U32), 0).then_inc(stage_zero, 1)
                nc.gpsimd.memset(stage_c[:, par, :].bitcast(U32), 0).then_inc(stage_zero, 1)
            nc.gpsimd.memset(v_diag[:, :, :, :, :], 0.0).then_inc(v_diag_zero, 1)
            ffn_small(0)
            ln_rstd(1)
            for t in range(NT):
                if t % 4 == 0:
                    pool.wait_ge(ln[1]["xhat"], t + 4)
                nc.gpsimd.tensor_tensor(x[:, t, :], x[:, t, :], bo_row[:, :], ALU.add).then_inc(x_bo, 1)

            def spread_v(h, par):
                for quad in range(4):
                    q = slice(32 * quad, 32 * quad + 32)
                    if isinstance(h, int) and h * 4 + quad == 0:
                        pool.wait_ge(x_bo, NT)
                    else:
                        pool.wait_ge(v_diag_ready, h * 4 + quad)
                    nc.gpsimd.tensor_copy(v_diag[q, par, :, quad, :],
                                          v_rep[q, :, bass.ds(h * HP, HP)]).then_inc(v_diag_ready, 1)

            pool.wait_ge(v_diag_zero, 1)
            pool.wait_ge(v_rep_in, 16 * 16)
            spread_v(0, 0)
            spread_v(1, 1)
            with pool.Fori(0, (H - 2) // 2) as it:
                for k in range(2):
                    pool.wait_ge(av_ready, it * 2 + (k + 1))
                    spread_v(it * 2 + (2 + k), k)
            pool.wait_ge(v_diag_ready, 4 * H)
            ln_rstd(2)
            ffn_small(1)

        @block.scalar
        def _(act):
            loads = [(w1_sb, w1_d.rearrange("(c p) d -> p c d", p=128)), (w2_sb, w2_d),
                     (ident[:, :], ident_d), (g1c, col(g1_d)), (lb1c, col(lb1_d)),
                     (b1row[:, :], row(b1_d, HID)), (b2_row, row(b2_d, D)), (bo_row[:, :], row(bo_d, D))]
            for c in range(HC):
                for dst, src in ((g2c, g2_d), (lb2c, lb2_d)):
                    loads.append((dst[:, c:c + 1], col(src[c * 128:(c + 1) * 128])))
            for dst, src in loads:
                act.dma_start(dst, src).then_inc(weights_in, 16)
            loads = ((wp_sb, wp_d), (embT, embT_d), (wq_sb, wq_d), (wk_sb, wk_d), (wv_sb, wv_d),
                     (wo_sb[:, :], wo_d), (bv_row, row(bv_d, D)), (bqc, col(bq_d)), (bkc, col(bk_d)),
                     (bpc, col(bp_d)), (uc, u_d.rearrange("a h b p -> (a b h p)").rearrange("(p a) -> p a", a=1)),
                     (vc, v_d.rearrange("a h b p -> (a b h p)").rearrange("(p a) -> p a", a=1)))
            for dst, src in loads:
                act.dma_start(dst, src).then_inc(qkv_weights_in, 16)

            act.wait_ge(weights_in, 16 * 16)
            act.wait_ge(ones_set, 1)
            for c in range(HC):
                nc.scalar.activation(lb2_rep[:, c, :], ones[:, :], ACT.Copy, scale=lb2c[:, c:c + 1])\
                    .then_inc(lb2_ready, 1)
            act.wait_ge(tern_turned, 1)
            nc.scalar.activation(w1T[:, :], ps[0][:, :], ACT.Copy, scale=wstep[:, 0:1]).then_inc(w1_ready, 1)

            def ln_evac(f):
                s = ln[f]
                for g in range(B):
                    act.wait_ge(s["turned"], 4 * g + 4)
                    dst, src = xT[:, g * 512:(g + 1) * 512], ps[6 + g % 2][:, :]
                    if f == 1:
                        nc.scalar.activation(dst, src, ACT.Copy).then_inc(s["xT"], 1)
                    else:
                        nc.scalar.activation(dst, src, ACT.Identity, scale=g1c, bias=lb1c).then_inc(s["xT"], 1)

            def ffn(f):
                s = ff[f]
                for n in range(NT + 3):
                    if n < NT:
                        act.wait_ge(s["hid_biased"], n + 1)
                        if n >= 3:
                            act.wait_ge(s["gnorm"], n - 2)
                        nc.scalar.activation(ge[:, n % 3, :], hs[:, n % 2, :], ACT.Gelu).then_inc(s["gelu"], 1)
                    t = n - 3
                    if t >= 0:
                        act.wait_ge(s["gturned"], t + 1)
                        if t >= 2:
                            act.wait_ge(s["ffn"], t - 1)
                        nc.scalar.activation(gT[:, t % 2, :], ps[2 + t % 2][:, :], ACT.Copy).then_inc(s["gT"], 1)

            ln_evac(0)
            act.wait_ge(qkv_weights_in, 16 * 12)
            act.wait_ge(pos_mm, 1)
            nc.scalar.activation(pf, ps[5][:, :], ACT.Identity, bias=bpc).then_inc(pos_f, 1)
            ffn(0)
            ln_evac(1)
            for b in range(B):
                act.wait_ge(q_mm, b + 1)
                act.wait_ge(bias_cols_ready, 2)
                if b:
                    act.wait_ge(q_split, b)
                    act.wait_ge(k_split, b)
                nc.scalar.activation(qf[:, 0, :], ps[0][:, :], ACT.Identity, scale=SCALE, bias=quc).then_inc(q_f, 1)
                nc.scalar.activation(qf[:, 1, :], ps[0][:, :], ACT.Identity, scale=SCALE, bias=qvc).then_inc(q_f, 1)
                act.wait_ge(k_mm, b + 1)
                nc.scalar.activation(kf, ps[1][:, :], ACT.Identity, bias=bkc).then_inc(k_f, 1)

            def exp_tile(h, q):
                act.wait_ge(max_ready, h * NQ + (q + 1))
                if not (isinstance(h, int) and h * NQ + q < 4):
                    act.wait_ge(pT_ready, h * NQ + (q - 3))
                nc.scalar.activation(probs[:, q % 4, :], ps[q % SB][:, :], ACT.Exp,
                                     bias=negmax[:, q % 8:q % 8 + 1],
                                     accum_out=rowsum[:, bass.ds(h * NQ + q, 1)]).then_inc(probs_ready, 1)

            def take_o(h, par, pair):
                act.wait_ge(av_ready, h + 1)
                if not (isinstance(h, int) and h < 2):
                    act.wait_ge(o_out[par], pair * 16)
                nc.scalar.activation(o_sb[:, par, :], ps[4 + par][:, 0:128], ACT.Copy).then_inc(o_ready, 1)

            for h in range(2):
                for q in range(NQ):
                    exp_tile(h, q)
            for h in range(2, 4):
                for q in range(NQ):
                    exp_tile(h, q)
                    if q == 3:
                        take_o(h - 2, h % 2, 0)
            with act.Fori(0, (H - 4) // 2) as it:
                for k in range(2):
                    for q in range(NQ):
                        exp_tile(it * 2 + (4 + k), q)
                        if q == 3:
                            take_o(it * 2 + (2 + k), k, it + 1)
            for h in (H - 2, H - 1):
                take_o(h, h % 2, H // 2 - 1)
            ln_evac(2)
            ffn(1)

        @block.vector
        def _(dve):
            steps = [0]

            def chain(ins):
                ins.then_inc(dve_step, 1)
                steps[0] += 1
                dve.wait_ge(dve_step, steps[0])

            def ln_stat(f, t):
                s = ln[f]
                x_made(dve, f, t)
                nc.vector.bn_stats(stat[:, t % 2, :], x[:, t, :]).then_inc(s["stat"], 1)
                dve.wait_ge(s["stat"], t + 1)
                nc.vector.bn_aggr(mv[:, t, :], stat[:, t % 2, :]).then_inc(s["mean"], 1)

            def ln_xhat(f, t):
                s = ln[f]
                dve.wait_ge(s["rstd"], t // 4 + 1)
                if t >= 4:
                    dve.wait_ge(s["turned"], t - 3)
                nc.vector.tensor_scalar(xh[:, t % 4, :], x[:, t, :], mv[:, t, 0:1], rs[:, t:t + 1],
                                        ALU.subtract, ALU.mult).then_inc(s["xhat"], 1)

            for t in range(NT):
                ln_stat(0, t)
            dve.wait_ge(weights_in, 16 * 16)
            nc.vector.tensor_reduce(wsum[:, 0:1], w1_sb, AX.XY, ALU.add,
                                    apply_absolute_value=True)
            nc.vector.tensor_reduce(wsum[:, 1:2], w2_sb, AX.X, ALU.add,
                                    apply_absolute_value=True).then_inc(wsum_ready, 1)
            dve.wait_ge(wtotal_ready, 1)
            chain(nc.vector.tensor_scalar(wclip, ps[4][:, 0:2], 1.0 / (D * HID), 1e-5, ALU.mult, ALU.max))
            chain(nc.vector.reciprocal(wscale, wclip))
            chain(nc.vector.reciprocal(wstep, wscale))
            for n, w in enumerate((w1_sb.rearrange("p c n -> p (c n)"), w2_sb)):
                sc = wscale[:, n:n + 1]
                nc.vector.tensor_scalar(tmp_t[:, 0, :], w, sc, 0.5, ALU.mult, ALU.is_gt)
                chain(nc.vector.tensor_scalar(tmp_t[:, 1, :], w, sc, -0.5, ALU.mult, ALU.is_lt))
                nc.vector.tensor_tensor(tern[:, n, :], tmp_t[:, 0, :], tmp_t[:, 1, :], ALU.subtract)\
                    .then_inc(tern_ready, 1)
                dve.wait_ge(tern_ready, n + 1)
            for t in range(NT):
                ln_xhat(0, t)
            dve.wait_ge(tern_turned, 2)
            for c in range(HC):
                nc.vector.tensor_scalar(w2T[:, c, :], ps[1][:, c * 128:(c + 1) * 128], wstep[:, 1:2], None,
                                        ALU.mult)
                ins = nc.vector.tensor_scalar(w2g[:, c, :], ps[1][:, c * 128:(c + 1) * 128], wstep[:, 1:2],
                                              g2c[:, c:c + 1], ALU.mult, ALU.mult)
            ins.then_inc(w2_ready, 1)
            dve.wait_ge(const_summed, 1)
            chain(nc.vector.tensor_tensor(half_const[:, :], ps[4][:, 0:128], b2_row, ALU.add))
            nc.vector.tensor_scalar(half_const[:, :], half_const[:, :], 0.5, None, ALU.mult)\
                .then_inc(const_ready, 1)
            dve.wait_ge(qkv_weights_in, 16 * 12)
            for dst, src in ((quc, uc), (qvc, vc)):
                chain(nc.vector.tensor_tensor(dst, bqc, src, ALU.add))
                nc.vector.tensor_scalar(dst, dst, SCALE, None, ALU.mult).then_inc(bias_cols_ready, 1)
            dve.wait_ge(pos_f, 1)
            dve.wait_ge(zs_zero, 1)
            chain(nc.vector.tensor_copy(zs[:, 0, 0:S], pf))
            nc.vector.tensor_copy(zs[:, 2, S + 1:2 * S], zs[:, 0, 0:S - 1]).then_inc(pos_split, 1)
            chain(nc.vector.tensor_tensor(zs[:, 1, 0:S], pf, zs[:, 0, 0:S], ALU.subtract))
            nc.vector.tensor_copy(zs[:, 3, S + 1:2 * S], zs[:, 1, 0:S - 1]).then_inc(pos_split, 1)

            def ffn(f, between=lambda t: None):
                s = ff[f]
                for n in range(NT + 6):
                    if n < NT:
                        dve.wait_ge(s["hid"], n + 1)
                        if n >= 2:
                            dve.wait_ge(s["gelu"], n - 1)
                        nc.vector.tensor_tensor(hs[:, n % 2, :], ps[n % 2][:, :], b1row[:, :], ALU.add)\
                            .then_inc(s["hid_biased"], 1)
                    t = n - 1
                    if 0 <= t < NT:
                        dve.wait_ge(s["gelu"], t + 1)
                        nc.vector.bn_stats(gstat[:, t % 2, :], ge[:, t % 3, :]).then_inc(s["gstat"], 1)
                    t = n - 4
                    if 0 <= t < NT:
                        dve.wait_ge(s["ffn"], t + 1)
                        dve.wait_ge(s["x_const"], t + 1)
                        nc.vector.scalar_tensor_tensor(x[:, t, :], ps[4 + t % 2][:, 0:128], 0.5, x[:, t, :],
                                                       ALU.mult, ALU.add).then_inc(s["x_new"], 1)
                    t = n - 1
                    if 0 <= t < NT:
                        dve.wait_ge(s["gstat"], t + 1)
                        nc.vector.bn_aggr(gmv[:, t, :], gstat[:, t % 2, :]).then_inc(s["gmean"], 1)
                    t = n - 2
                    if 0 <= t < NT:
                        dve.wait_ge(s["grstd"], t + 1)
                        if t >= 2:
                            dve.wait_ge(s["gturned"], t - 1)
                        nc.vector.tensor_scalar(gn[:, t % 2, :], ge[:, t % 3, :], gmv[:, t, 0:1],
                                                grs[:, t:t + 1], ALU.subtract, ALU.mult).then_inc(s["gnorm"], 1)
                    if 0 <= n - 5 < NT:
                        between(n - 5)

            ffn(0, lambda t: ln_stat(1, t))
            for t in range(NT):
                ln_xhat(1, t)
            tok = lambda ap: ap.rearrange("p (g i) -> p i g", i=NI)
            for b in range(B):
                c = slice(b * S, (b + 1) * S)
                for n, (hi, lo) in enumerate(((uh, ul), (vh, vl))):
                    dst = lambda a: a[:, c].rearrange("p (i g) -> p i g", i=NI)
                    dve.wait_ge(q_f, 2 * b + n + 1)
                    nc.vector.tensor_copy(dst(hi), tok(qf[:, n, :])).then_inc(q_high, 1)
                    dve.wait_ge(q_high, 2 * b + n + 1)
                    ins = nc.vector.tensor_tensor(dst(lo), tok(qf[:, n, :]), dst(hi), ALU.subtract)
                ins.then_inc(q_split, 1)
                dve.wait_ge(k_f, b + 1)
                nc.vector.tensor_copy(kh[:, c], kf).then_inc(k_high, 1)
                dve.wait_ge(k_high, b + 1)
                nc.vector.tensor_tensor(kl[:, c], kf, kh[:, c], ALU.subtract).then_inc(k_split, 1)
                for t in range(4 * b, 4 * b + 4):
                    dve.wait_ge(v_mm, t + 1)
                    nc.vector.tensor_tensor(v_sb[:, t, :], ps[2 + t % 2][:, 0:128], bv_row, ALU.add)\
                        .then_inc(v_ready, 1)

            dve.wait_ge(scratch_out, 16 * (6 + B * 17))
            dve.wait_ge(v_rep_in, 16 * 16)

            def row_max(h, q):
                dve.wait_ge(scores_ready, h * NQ + (q + 1))
                nc.vector.tensor_reduce(negmax[:, q % 8:q % 8 + 1], ps[q % SB][:, :], AX.X, ALU.max,
                                        negate=True).then_inc(max_ready, 1)

            def turn(h, par, q):
                dve.wait_ge(probs_ready, h * NQ + (q + 1))
                if q == 0 and not (isinstance(h, int) and h < 2):
                    dve.wait_ge(av_ready, h - 1)
                nc.vector.transpose(pT[:, par, q, :], probs[:, q % 4, :]).then_inc(pT_ready, 1)

            def head(h, par, first=False):
                for q in range(NQ):
                    row_max(h, q)
                    if q >= 2:
                        turn(h, par, q - 2)
                    elif not first:
                        turn(h - 1, 1 - par, NQ - 2 + q)

            head(0, 0, True)
            head(1, 1)
            with dve.Fori(0, (H - 2) // 2) as it:
                for k in range(2):
                    head(it * 2 + (2 + k), k)
            turn(H - 1, 1, NQ - 2)
            turn(H - 1, 1, NQ - 1)

            dve.wait_ge(probs_ready, H * NQ)
            dve.wait_ge(av_ready, H)
            nc.vector.reciprocal(rec, rowsum[:, :]).then_inc(rec_ready, 1)
            dve.wait_ge(rec_ready, 1)
            src = rec.rearrange("p (h q) -> p q h", q=NQ)
            for e in range(HP):
                ins = nc.vector.tensor_copy(recx[:, :, :, e], src)
            ins.then_inc(recx_ready, 1)
            dve.wait_ge(attn_in, 16)
            av = attnT.rearrange("p (b j q i) -> p q j b i", b=B, j=4, q=NQ)
            for q in range(NQ):
                dve.wait_ge(rec_turned, q // 4 + 1)
                r = ps[q // 4][:, (q % 4) * 128:(q % 4 + 1) * 128].rearrange("p (j b i) -> p j b i", j=4, b=B)
                ins = nc.vector.tensor_tensor(av[:, q], av[:, q], r, ALU.mult)
            ins.then_inc(attn_scaled, 1)
            for t in range(NT):
                dve.wait_ge(wo_mm, t + 1)
                dve.wait_ge(x_bo, t + 1)
                nc.vector.tensor_tensor(x[:, t, :], x[:, t, :], ps[4 + t % 2][:, 0:128], ALU.add)\
                    .then_inc(x_attn, 1)
                ln_stat(2, t)
            for t in range(NT):
                ln_xhat(2, t)
            ffn(1)

        @block.tensor
        def _(pe):
            mm = nc.tensor.matmul
            pe.wait_ge(ones_set, 1)
            pe.wait_ge(wsum_ready, 1)
            mm(ps[4][:, 0:2], ones[:, :], wsum, start=True, stop=True).then_inc(wtotal_ready, 1)
            pe.wait_ge(weights_in, 16 * 16)
            for n in range(2):
                pe.wait_ge(tern_ready, n + 1)
                for c in range(HC):
                    ins = nc.tensor.transpose(ps[n][:, c * 128:(c + 1) * 128],
                                              tern[:, n, c * 128:(c + 1) * 128], ident[:, :])
                ins.then_inc(tern_turned, 1)

            def ln_turn(f):
                s = ln[f]
                for t in range(NT):
                    g = t // 4
                    pe.wait_ge(s["xhat"], t + 1)
                    if g >= 2:
                        pe.wait_ge(s["xT"], g - 1)
                    nc.tensor.transpose(ps[6 + g % 2][:, (t % 4) * 128:(t % 4 + 1) * 128], xh[:, t % 4, :],
                                        ident[:, :]).then_inc(s["turned"], 1)

            def ffn(f):
                s = ff[f]
                for n in range(NT + 4):
                    if n < NT:
                        pe.wait_ge(ln[2 * f]["xT"], n // 4 + 1)
                        if n >= 2:
                            pe.wait_ge(s["hid_biased"], n - 1)
                        mm(ps[n % 2][:, :], xT[:, n * 128:(n + 1) * 128], w1T[:, :],
                           start=True, stop=True).then_inc(s["hid"], 1)
                    t = n - 3
                    if 0 <= t < NT:
                        pe.wait_ge(s["gnorm"], t + 1)
                        if t >= 2:
                            pe.wait_ge(s["gT"], t - 1)
                        for c in range(HC):
                            ins = nc.tensor.transpose(ps[2 + t % 2][:, c * 128:(c + 1) * 128],
                                                      gn[:, t % 2, c * 128:(c + 1) * 128], ident[:, :])
                        ins.then_inc(s["gturned"], 1)
                    t = n - 4
                    if 0 <= t < NT:
                        pe.wait_ge(s["gT"], t + 1)
                        if t >= 2:
                            pe.wait_ge(s["x_new"], t - 1)
                        for c in range(HC):
                            ins = mm(ps[4 + t % 2][:, 0:128], gT[:, t % 2, c * 128:(c + 1) * 128],
                                     w2g[:, c, :], start=(c == 0), stop=(c == HC - 1))
                        ins.then_inc(s["ffn"], 1)

            ln_turn(0)
            pe.wait_ge(w2_ready, 1)
            pe.wait_ge(lb2_ready, HC)
            for c in range(HC):
                ins = mm(ps[4][:, 0:128], lb2_rep[:, c, :], w2T[:, c, :], start=(c == 0), stop=(c == HC - 1))
            ins.then_inc(const_summed, 1)
            pe.wait_ge(qkv_weights_in, 16 * 12)
            mm(ps[5][:, :], wp_sb, embT, start=True, stop=True).then_inc(pos_mm, 1)
            pe.wait_ge(w1_ready, 1)
            pe.wait_ge(const_ready, 1)
            pe.wait_ge(pos_f, 1)
            ffn(0)
            ln_turn(1)
            pe.wait_ge(ff[0]["x_new"], NT)
            for b in range(B):
                pe.wait_ge(ln[1]["xT"], b + 1)
                c = slice(b * S, (b + 1) * S)
                if b:
                    pe.wait_ge(q_f, 2 * b)
                    pe.wait_ge(k_f, b)
                mm(ps[0][:, :], wq_sb, xT[:, c], start=True, stop=True).then_inc(q_mm, 1)
                mm(ps[1][:, :], wk_sb, xT[:, c], start=True, stop=True).then_inc(k_mm, 1)
                for t in range(4 * b, 4 * b + 4):
                    if t >= 2:
                        pe.wait_ge(v_ready, t - 1)
                    mm(ps[2 + t % 2][:, 0:128], xT[:, t * 128:(t + 1) * 128], wv_sb,
                       start=True, stop=True).then_inc(v_mm, 1)
            pe.wait_ge(v_ready, NT)
            pe.wait_ge(q_f, 2 * B)
            pe.wait_ge(k_f, B)

            def scores(h, par, q):
                if not (isinstance(h, int) and h * NQ + q < SB):
                    pe.wait_ge(probs_ready, h * NQ + (q + 1 - SB))
                bank = ps[q % SB]

                def rows(a, j):
                    return a.rearrange("k (b g) -> k b g", g=NG)[:, :, j * NQ + q]

                for j in range(4):
                    o = bank[32 * j:32 * j + 32, :]
                    mm(o, rows(stage_c[:, par, :], j), stage_k[:, par, :], start=True, stop=False,
                       skip_group_check=True)
                for j in range(4):
                    a0 = 128 * j + NI * q
                    o = bank[32 * j:32 * j + 32, :]
                    m0 = S - NI - a0
                    mm(o, rows(stage_q[:, par, 0, :], j), stage_z[:, par, 0, m0:m0 + S], start=False,
                       stop=False, skip_group_check=True)
                for j in range(4):
                    a0 = 128 * j + NI * q
                    n = a0 + NI
                    m0 = S - NI - a0
                    mm(bank[32 * j:32 * j + 32, 0:n], rows(stage_q[:, par, 1, :], j),
                       stage_z[:, par, 1, m0:m0 + n], start=False, stop=False, skip_group_check=True)
                for j in range(4):
                    a0 = 128 * j + NI * q
                    m0 = S - NI - a0
                    ins = mm(bank[32 * j:32 * j + 32, a0 + 2:S], rows(stage_q[:, par, 2, :], j),
                             stage_z[:, par, 2, m0 + a0 + 2:m0 + S], start=False, stop=True,
                             skip_group_check=True)
                ins.then_inc(scores_ready, 1)

            def values(h, par, kb):
                if kb == 0:
                    pe.wait_ge(pT_ready, (h + 1) * NQ)
                    pe.wait_ge(v_diag_ready, (h + 1) * 4)
                    if not (isinstance(h, int) and h < 2):
                        pe.wait_ge(o_ready, h - 1)
                for b in range(B):
                    mov = pT[:, par, :, 32 * kb + NI * b:32 * kb + NI * (b + 1)]
                    ins = mm(ps[4 + par][32 * b:32 * b + 32, 0:128],
                             v_diag[:, par, b * KB + kb, :, :].rearrange("p j e -> p (j e)"), mov,
                             start=(kb == 0), stop=(kb == KB - 1), skip_group_check=True)
                if kb == KB - 1:
                    ins.then_inc(av_ready, 1)

            def head(h, par, staged_count, first=False):
                pe.wait_ge(staged[par], staged_count)
                for q in range(NQ):
                    scores(h, par, q)
                    if not first and q >= 3:
                        values(h - 1, 1 - par, q - 3)
                if not first:
                    for kb in range(NQ - 3, KB):
                        values(h - 1, 1 - par, kb)

            head(0, 0, 16 * LOADS, True)
            head(1, 1, 16 * LOADS)
            head(2, 0, 2 * 16 * LOADS)
            with pe.Fori(0, (H - 4) // 2) as it:
                for k in range(2):
                    head(it * 2 + (3 + k), 1 - k, (it + (2 + k)) * (16 * LOADS))
            head(H - 1, 1, (H // 2) * 16 * LOADS)
            for kb in range(KB):
                values(H - 1, 1, kb)

            pe.wait_ge(recx_ready, 1)
            for q in range(NQ):
                ins = mm(ps[q // 4][:, (q % 4) * 128:(q % 4 + 1) * 128],
                         recx[:, q, :, :].rearrange("p h e -> p (h e)"), ident[:, :], start=True, stop=True)
                if q % 4 == 3:
                    ins.then_inc(rec_turned, 1)
            pe.wait_ge(attn_scaled, 1)
            pe.wait_ge(o_ready, H)
            for t in range(NT):
                if t >= 2:
                    pe.wait_ge(x_attn, t - 1)
                mm(ps[4 + t % 2][:, 0:128], attnT[:, t * 128:(t + 1) * 128], wo_sb[:, :],
                   start=True, stop=True).then_inc(wo_mm, 1)
            ln_turn(2)
            pe.wait_ge(x_attn, NT)
            ffn(1)


_INS = ["x", "Wq", "bq", "Wk", "bk", "Wv", "bv", "Wp", "bp", "Wo", "bo", "u", "v"]
_FFN = ["ln1_g", "ln1_b", "w1", "b1", "ln2_g", "ln2_b", "w2", "b2"]


def kernel(**inputs):
    import concourse.bacc as bacc
    from concourse.bass_utils import run_bass_kernel_spmd

    pos = np.arange(S, dtype=np.float32)
    idx = np.arange(D // 2, dtype=np.float32)
    inv_freq = (np.float32(1.0) / np.float32(10000.0) ** (np.float32(2.0) * idx / np.float32(D))).astype(np.float32)
    ang = pos[:, None] * inv_freq[None, :]
    emb = np.concatenate([np.sin(ang), np.cos(ang)], axis=-1).astype(np.float32)

    nc = bacc.Bacc("TRN2", target_bir_lowering=False, num_devices=1)
    arrays, args = {}, []
    named = [(n, inputs["L0_attn_" + n]) for n in _INS] + [(n, inputs["L0_ffn_" + n]) for n in _FFN]
    named += [("embT", emb.T), ("ident", np.eye(128, dtype=np.float32))]
    for name, a in named:
        a = np.ascontiguousarray(a)
        arrays[f"in_{name}"] = a
        args.append(nc.dram_tensor(f"in_{name}", a.shape, mybir.dt.from_np(a.dtype), kind="ExternalInput").ap())
    out = nc.dram_tensor("out_0", (B, S, D), F32, kind="ExternalOutput").ap()
    macaron_kernel(nc, args, out)
    r = run_bass_kernel_spmd(nc, [arrays], core_ids=[0])
    return r.results[0]["out_0"]
```

```python
from contextlib import ExitStack

import numpy as np

import concourse.bass as bass
from concourse import mybir

F32 = mybir.dt.float32
F16 = mybir.dt.float16
U32 = mybir.dt.uint32
ALU = mybir.AluOpType
ACT = mybir.ActivationFunctionType
AX = mybir.AxisListType

B, S, D = 4, 512, 128
H, HP = 16, 8
HID = 512
NT = B * S // 128
HC = HID // 128
NI = 8
NQ = S // 4 // NI
NG = S // NI
KB = S // 32
EPS = 1e-5
SCALE = float(HP) ** -0.5
NP = NQ // 2
ZW = 2 * S - NI
ZB0 = S - NI + 2
STEPS = (30, 23)
TURN_STEPS = {1: 1, 5: 2, 8: 3}
XHAT1_STEPS = {13: 0, 17: 1, 21: 2, 24: 3}
TURN1_STEPS = {14: 0, 18: 1, 22: 2, 25: 3}
QK_STEPS = {17: 0, 21: 1, 23: 2, 27: 3}
VW = S + S // NI
LOADS_FIRST = 5
LOADS = 16


def macaron_kernel(nc, ins, out):
    x_d, w12_d, vectors_d, rows_d, wqkv_d, wo_d, wp_emb_d, ident_d = ins

    qs_dram = nc.dram_tensor("qs_scratch", (D, 2, 3, B * S), F16, kind="Internal").ap()
    qc_dram = nc.dram_tensor("qc_scratch", (D, 4, B * S), F16, kind="Internal").ap()
    kc_dram = nc.dram_tensor("kc_scratch", (D, 4, B, S), F16, kind="Internal").ap()
    z_dram = nc.dram_tensor("z_scratch", (D, 2, 3, 2 * S), F16, kind="Internal").ap()
    at_dram = nc.dram_tensor("attn_scratch", (H, HP, 16, 128), F32, kind="Internal").ap()

    with ExitStack() as ctx:
        def sb(name, shape, dt=F32):
            return ctx.enter_context(nc.sbuf_tensor(name, shape, dt))

        def sem(name):
            return ctx.enter_context(nc.semaphore(name))

        x = sb("x", [128, NT, D])
        xT = sb("xT", [128, B * S])
        xh = sb("xh", [128, 4, D])
        ident = sb("ident", [128, 128])
        ones = sb("ones", [128, 128])
        w1T = sb("w1T", [128, HID], F16)
        w2c = sb("w2c", [128, HC, D + 1])
        mean16 = sb("mean16", [128, 1], F16)
        half_const = sb("half_const", [128, D])
        rows = sb("rows", [128, 3, D])
        wo_sb = sb("wo_sb", [128, D])
        vectors = sb("vectors", [128, 19])
        cols = sb("cols", [128, 32])
        minus_half = sb("minus_half", [128, 8])
        stat = sb("stat", [128, 2, 6])
        mv = sb("mv", [128, NT, 2])
        rs = sb("rs", [128, NT])
        gmean = sb("gmean", [128, NT])
        gvar = sb("gvar", [128, NT])
        grs = sb("grs", [128, NT])
        stage_q = sb("stage_q", [128, 2, 3, B * S], F16)
        stage_c = sb("stage_c", [128, 2, B * S], F16)
        stage_k = sb("stage_k", [128, 2, S], F16)
        stage_z = sb("stage_z", [128, 2, 3, ZW], F16)
        probs = sb("probs", [128, 4, S])
        negmax = sb("negmax", [128, 8])
        rowsum = sb("rowsum", [128, H * NQ])
        pT = sb("pT", [128, 2, NQ, S])
        v_rep = sb("v_rep", [128, B * KB, D])
        v_diag = sb("v_diag", [128, 2, B * KB, 4, HP])
        o_sb = sb("o_sb", [128, 2, 128])
        pairs = [ctx.enter_context(nc.psum_tensor(f"pair{i}", [128, 2, 512], F32)) for i in range(4)]
        ps = [pairs[i // 2][:, i % 2, :] for i in range(8)]

        pTf = pT[:, :, :, :].rearrange("p a q s -> p (a q s)")
        wq_sb, wk_sb, wv_sb, wp_sb = (pTf[:, 128 * n:128 * n + 128] for n in range(4))
        embT = pTf[:, 512:1024]
        wq_s = pTf[:, 2048:2176]
        w2g = pTf[:, 2176:2688].rearrange("p (c n) -> p c n", c=HC)
        w2b = pTf[:, 2688:3200].rearrange("p (c n) -> p c n", c=HC)
        pf = pTf[:, 3584:4096]
        half = pTf[:, 4096:8192].bitcast(F16).rearrange("p (a n) -> p a n", a=4)
        uh, ul, kh, kl = (half[:, n, :] for n in range(4))
        vl = pTf[:, 8192:8192 + B * VW // 2].bitcast(F16).rearrange("p (b n) -> p b n", b=B)
        vh = pTf[:, 14336:14336 + B * VW // 2].bitcast(F16).rearrange("p (b n) -> p b n", b=B)
        zs = pTf[:, 10240:12288].bitcast(F16).rearrange("p (a n) -> p a n", a=4)
        v_sb = pTf[:, 12288:14336].rearrange("p (t n) -> p t n", t=NT)
        w1_sb = pTf[:, 14336:14848].rearrange("p (c n) -> p c n", c=HC)
        w2_sb = pTf[:, 14848:15360]
        tern = pTf[:, 15360:16384].rearrange("p (a n) -> p a n", a=2)
        tmp_t = pTf[:, 4096:5120].rearrange("p (a n) -> p a n", a=2)
        vrf = v_rep[:, :, :].rearrange("p a n -> p (a n)")
        xT_high, xT_low = (vrf[:, n:n + 1024].bitcast(F16) for n in (0, 1024))
        ge = vrf[:, 2048:6144].rearrange("p (a n) -> p a n", a=8)
        sq = vrf[:, 6144:7168].rearrange("p (a n) -> p a n", a=2)
        sqsum = vrf[:, 7168:7680]
        sq_high, sq_low = (vrf[:, n:n + 256].bitcast(F16) for n in (7680, 7936))
        attnT = xT[:, :]
        rec = pTf[:, 2048:2304]
        recx = pTf[:, 4096:6144].rearrange("p (q h e) -> p q h e", q=NQ, h=H)

        g1c, lb1c, bqc, uc, vc, bkc, bpc = (vectors[:, n:n + 1] for n in range(7))
        g2c, lb2c, b1c = (vectors[:, n:n + HC] for n in (7, 11, 15))
        b2_row, bo_row, bv_row = (rows[:, n, :] for n in range(3))
        quc, qvc = cols[:, 0:1], cols[:, 1:2]
        wsum, wclip, wscale, wstep = (cols[:, n:n + 2] for n in (2, 4, 6, 8))
        half_step = cols[:, 10:11]
        gelu_b1 = cols[:, 12:12 + HC]
        pivot_sum = cols[:, 16:17]
        minus_pivot = cols[:, 17:18]

        x_in = [sem(f"x_in{b}") for b in range(B)]
        w_in = sem("w_in")
        vectors_in = sem("vectors_in")
        rows_in = sem("rows_in")
        pos_weights_in = sem("pos_weights_in")
        ident_in = sem("ident_in")
        qkv_weights_in = sem("qkv_weights_in")
        wo_in = sem("wo_in")
        step_ready = sem("step_ready")
        half_step_ready = sem("half_step_ready")
        gelu_b1_ready = sem("gelu_b1_ready")
        pivot_summed = sem("pivot_summed")
        pivot_ready = sem("pivot_ready")
        wq_scaled = sem("wq_scaled")
        ones_set = sem("ones_set")
        wsum_ready = sem("wsum_ready")
        wtotal_ready = sem("wtotal_ready")
        dve_step = sem("dve_step")
        tern_ready = sem("tern_ready")
        tern_turned = sem("tern_turned")
        w1_ready = sem("w1_ready")
        w2g_ready = sem("w2g_ready")
        w2b_ready = sem("w2b_ready")
        w2_summed = sem("w2_summed")
        w2_ready = sem("w2_ready")
        const_summed = sem("const_summed")
        const_ready = sem("const_ready")
        bias_cols_ready = sem("bias_cols_ready")
        stage_zero = sem("stage_zero")
        ln = [{n: sem(f"{n}{f}") for n in ("stat", "mean", "rstd0_", "rstd", "xhat", "turned", "xT", "xT_low")}
              for f in range(3)]
        ff = [{n: sem(f"{n}{f}") for n in ("hid", "gelu", "squared", "sq_summed", "sq_split", "sq_mean",
                                          "gmean", "gmean_sq", "gvar", "gvar_eps", "grstd", "ffn",
                                          "x_const", "x_new")}
              for f in range(2)]
        pos_mm = sem("pos_mm")
        pos_f = sem("pos_f")
        pos_split = sem("pos_split")
        zs_zero = sem("zs_zero")
        q_mm = sem("q_mm")
        k_mm = sem("k_mm")
        v_mm = sem("v_mm")
        q_high = sem("q_high")
        q_split = sem("q_split")
        v_extended = sem("v_extended")
        k_high = sem("k_high")
        k_split = sem("k_split")
        v_ready = sem("v_ready")
        v_rep_in = sem("v_rep_in")
        z_out = sem("z_out")
        c_out = [sem(f"c_out{b}") for b in range(B)]
        q_out = sem("q_out")
        staged = [sem("staged_even"), sem("staged_odd")]
        staged_first = sem("staged_first")
        v_diag_ready = sem("v_diag_ready")
        v_diag_zero = sem("v_diag_zero")
        scores_ready = sem("scores_ready")
        max_ready = sem("max_ready")
        probs_ready = sem("probs_ready")
        pT_ready = sem("pT_ready")
        av_ready = sem("av_ready")
        o_ready = sem("o_ready")
        o_out = [sem("o_out_even"), sem("o_out_odd")]
        attn_in = sem("attn_in")
        rec_ready = sem("rec_ready")
        recx_ready = sem("recx_ready")
        rec_turned = sem("rec_turned")
        attn_scaled = sem("attn_scaled")
        wo_mm = sem("wo_mm")
        x_bo = sem("x_bo")
        x_attn = sem("x_attn")
        out_done = sem("out_done")

        def x_made(eng, f, t):
            if f == 0:
                eng.wait_ge(x_in[t // 4], 16)
            elif f == 1:
                eng.wait_ge(ff[0]["x_new"], t + 1)
            else:
                eng.wait_ge(x_attn, t // 4 + 1)

        block = ctx.enter_context(nc.Block())

        def sums(m):
            g, c = divmod(m, HC)
            return (HC - 1) * g + max(c, 1)

        def moments(g):
            return pairs[1 + g % 2]

        def out_tile(t):
            return moments(t // 4)[:, t % 4 // 2, t % 2 * (D + 1):(t % 2 + 1) * (D + 1)]

        SQ0 = 2 * (D + 1) + 2

        def ln_bank(f, g):
            return 6 + g % 2

        def by_row(n, dst, src):
            if n == 0:
                return (dst.rearrange("p (j i g) -> p j i g", j=4, i=NI),
                        src.rearrange("p (j g i) -> p j i g", j=4, i=NI))
            return dst.rearrange("p (i g) -> p i g", i=NI), src.rearrange("p (g i) -> p i g", i=NI)

        def stage_content(eng, h, par, b, done):
            c_rows = qc_dram.rearrange("(h p) t n -> h (p t) n", p=HP)[h]
            dst = stage_c[32 * b:32 * b + 32, par, :].rearrange("r (j b m) -> r j b m", j=4, b=B)[:, :, b]
            src = c_rows[:, b * S:(b + 1) * S].rearrange("r (j m) -> r j m", j=4)
            eng.dma_start(dst, src).then_inc(done, 16)

        def stage_keys(eng, h, par, done):
            k_rows = kc_dram.rearrange("(h p) t b n -> h b (p t) n", p=HP)[h]
            eng.dma_start(stage_k[:, par, :], k_rows).then_inc(done, 16)

        def rep_ap(view, dims):
            return bass.AP(view.tensor, view.offset, [list(view.ap[0])] + [list(d) for d in dims])

        @block.sync
        def _(sp):
            xv = x_d.rearrange("b (t p) d -> b p t d", p=128)
            for b in range(B):
                sp.dma_start(x[:, 4 * b:4 * b + 4, :], xv[b]).then_inc(x_in[b], 16)
            sp.dma_start(pTf[:, 384:1024], wp_emb_d).then_inc(pos_weights_in, 16)
            sp.dma_start(pTf[:, 0:384], wqkv_d).then_inc(qkv_weights_in, 16)
            sp.dma_start(wo_sb[:, :], wo_d).then_inc(wo_in, 16)
            sp.wait_ge(pos_split, 2)
            for t, kind, src in ((0, 0, 0), (1, 0, 2), (0, 1, 0), (1, 1, 1), (0, 2, 2), (1, 2, 3)):
                sp.dma_start(z_dram[:, t, kind, :], zs[:, src, :]).then_inc(z_out, 16)

            def stage_pos(h, par):
                z_rows = z_dram.rearrange("(h p) t k n -> h (p t) k n", p=HP)[h]
                for kind, lo, hi in ((0, 0, ZW), (1, 0, S), (2, ZB0, ZW)):
                    zr = z_rows[:, kind, :]
                    src = bass.AP(zr.tensor, zr.offset + lo, [[1, NI]] + [list(zr.ap[0])] + [[1, hi - lo]])
                    sp.dma_start(stage_z[:, par, kind, lo:hi], src).then_inc(staged[par], 16)

            def stage_queries(h, par):
                q_rows = qs_dram.rearrange("(h p) t k n -> h (p t) k n", p=HP)[h]
                for ii in range(NI):
                    i = NI - 1 - ii
                    src = q_rows.rearrange("r k (b m) -> r (k b) m", b=B)[:, :, i * NG:(i + 1) * NG]
                    dst = stage_q[16 * ii:16 * ii + 16, par, :, :].rearrange(
                        "r k (b m) -> r (k b) m", b=B)[:, :, i * NG:(i + 1) * NG]
                    sp.dma_start(dst, src).then_inc(staged[par], 16)

            sp.wait_ge(z_out, 16 * 6)
            stage_pos(0, 0)
            stage_pos(1, 1)
            for b in range(B):
                c = slice(b * S, (b + 1) * S)
                sp.wait_ge(v_extended, b + 1)
                sp.dma_start(qs_dram[:, :, 0, c], rep_ap(vl[:, b, :], [(NG, 2), (1, S)])).then_inc(q_out, 16)
                sp.dma_start(qs_dram[:, :, 1, c], rep_ap(vh[:, b, :], [(0, 2), (1, S)])).then_inc(q_out, 16)
                sp.dma_start(qs_dram[:, :, 2, c], rep_ap(vh[:, b, NG:], [(0, 2), (1, S)])).then_inc(q_out, 16)
                sp.wait_ge(q_split, 2 * b + 2)
                for t, src in ((0, uh), (2, ul)):
                    sp.dma_start(qc_dram[:, t:t + 2, c], rep_ap(src[:, c], [(0, 2), (1, S)]))\
                        .then_inc(c_out[b], 16)
                sp.wait_ge(k_split, b + 1)
                for t in (0, 2):
                    sp.dma_start(kc_dram[:, t:t + 2, b, :], rep_ap(kh[:, c], [(B * S, 2), (1, S)]))\
                        .then_inc(c_out[b], 16)
            sp.wait_ge(q_out, 16 * 3 * B)
            sp.wait_ge(stage_zero, 8)
            stage_queries(0, 0)
            sp.wait_ge(ff[0]["x_new"], NT)
            sp.wait_ge(v_ready, B)
            vr = v_rep[:, :, :].rearrange("p (t k) n -> p t k n", k=4)
            for quad in range(4):
                for kq in range(4):
                    sp.dma_start(vr[32 * quad:32 * quad + 32, :, kq, :],
                                 v_sb[32 * kq:32 * kq + 32, :, :]).then_inc(v_rep_in, 16)
            for b in range(B):
                sp.wait_ge(c_out[b], 64)
                stage_content(sp, 1, 1, b, staged[1])
            stage_keys(sp, 1, 1, staged[1])
            stage_queries(1, 1)

            def stage(h, par):
                stage_pos(h, par)
                for b in range(B):
                    stage_content(sp, h, par, b, staged[par])
                stage_keys(sp, h, par, staged[par])
                stage_queries(h, par)

            sp.wait_ge(scores_ready, NP)
            stage(2, 0)

            def send_o(h, par):
                sp.wait_ge(o_ready, h + 1)
                sp.dma_start(at_dram[h].rearrange("p j n -> j p n"),
                             o_sb[:, par, :]).then_inc(o_out[par], 16)

            with sp.Fori(0, (H - 4) // 2) as it:
                for k in range(2):
                    par = (3 + k) % 2
                    sp.wait_ge(scores_ready, (it * 2 + (2 + k)) * NP)
                    stage(it * 2 + (3 + k), par)
                    send_o(it * 2 + k, k)
            sp.wait_ge(scores_ready, (H - 2) * NP)
            stage(H - 1, 1)
            def read_o(h):
                sp.dma_start(attnT[HP * h:HP * h + HP, :], at_dram[h]).then_inc(attn_in, 16)

            for h in (H - 4, H - 3):
                send_o(h, h % 2)
            for par in range(2):
                sp.wait_ge(o_out[par], 16 * (H // 2 - 1))
            for h in range(H - 2):
                read_o(h)
            for h in (H - 2, H - 1):
                send_o(h, h % 2)
                sp.wait_ge(o_out[h % 2], 16 * (H // 2))
                read_o(h)
            ov = out.rearrange("b (t p) d -> (b t) p d", p=128)
            for t in range(NT):
                sp.wait_ge(ff[1]["x_new"], t + 1)
                sp.dma_start(ov[t], x[:, t, :]).then_inc(out_done, 16)
            sp.wait_ge(out_done, 16 * NT)

        @block.gpsimd
        def _(pool):
            nc.gpsimd.memset(ones[:, :], 1.0).then_inc(ones_set, 1)
            nc.gpsimd.memset(minus_half[:, :], -0.5).then_inc(ones_set, 1)
            nc.gpsimd.memset(mean16[:, :], 1.0 / HID).then_inc(ones_set, 1)
            nc.gpsimd.memset(w2c[:, :, D:D + 1], 1.0 / HID).then_inc(ones_set, 1)
            pool.wait_ge(ones_set, 4)
            nc.gpsimd.memset(zs[:, :, :].bitcast(U32), 0).then_inc(zs_zero, 1)
            nc.gpsimd.memset(stage_c[:, 0, :].bitcast(U32), 0).then_inc(stage_zero, 1)

            def ln_rstd(f, g, groups=1):
                s = ln[f]
                tiles = slice(4 * g, 4 * (g + groups))
                var, r = mv[:, tiles, 1], rs[:, tiles]
                pool.wait_ge(s["mean"], tiles.stop)
                m, a = (1.0, EPS) if f == 1 else (1 + EPS, EPS * EPS)
                nc.gpsimd.tensor_scalar(r, var, m, a, ALU.mult, ALU.add).then_inc(s["rstd0_"], groups)
                pool.wait_ge(s["rstd0_"], g + groups)
                nc.gpsimd.tensor_tensor(r, r, minus_half[:, 0:4 * groups], ALU.pow).then_inc(s["rstd"], groups)

            def ln_low(f, g):
                s = ln[f]
                c = slice(g * 512, (g + 1) * 512)
                pool.wait_ge(s["xT"], 2 * g + 2)
                nc.gpsimd.tensor_tensor(xT_low[:, c], xT[:, c], xT_high[:, c], ALU.subtract)\
                    .then_inc(s["xT_low"], 1)

            def zero_stage(par, n):
                if n == 3:
                    nc.gpsimd.memset(stage_c[:, par, :].bitcast(U32), 0).then_inc(stage_zero, 1)
                else:
                    nc.gpsimd.memset(stage_q[:, par, n, :].bitcast(U32), 0).then_inc(stage_zero, 1)

            def ffn(f):
                s = ff[f]
                for n in range(STEPS[f]):
                    if n in TURN_STEPS:
                        ln_low(2 * f, TURN_STEPS[n])
                    if n in (1, 4):
                        ln_rstd(2 * f, (1, 4).index(n) + 2)
                    g = (n - 2) // 4
                    if n % 4 == 2 and g < B:
                        pool.wait_ge(ln[2 * f]["xhat"], 4 * g + 4)
                        if n == 2 and f == 0:
                            pool.wait_ge(const_ready, 1)
                        part = x[:, 4 * g:4 * g + 4, :]
                        nc.gpsimd.tensor_tensor(part, part, rep_ap(half_const[:, :], [(0, 4), (1, D)]), ALU.add)\
                            .then_inc(s["x_const"], 1)
                    g = (n - 9) // 4
                    if n % 4 == 1 and 0 <= g < B:
                        r, v = grs[:, 4 * g:4 * g + 4], gvar[:, 4 * g:4 * g + 4]
                        pool.wait_ge(s["gvar"], g + 1)
                        nc.gpsimd.tensor_scalar(r, v, 0.0, EPS, ALU.max, ALU.add).then_inc(s["gvar_eps"], 1)
                        pool.wait_ge(s["gvar_eps"], g + 1)
                        nc.gpsimd.tensor_tensor(r, r, minus_half[:, 0:4], ALU.pow).then_inc(s["grstd"], 1)
                    if f == 1:
                        continue
                    if n % 4 == 2 and 0 <= (n - 10) // 4 < B:
                        ln_rstd(1, (n - 10) // 4)
                    if n in (6, 7, 9):
                        zero_stage(0, (6, 7, 9).index(n))
                    if n in (10, 12, 14, 16):
                        zero_stage(1, (10, 12, 14, 16).index(n))
                    if n == 18:
                        nc.gpsimd.memset(v_diag[:, :, :, :, :], 0.0).then_inc(v_diag_zero, 1)
                    if n in (23, 25, 28):
                        b = (23, 25, 28).index(n)
                        pool.wait_ge(c_out[b], 64)
                        stage_content(pool, 0, 0, b, staged_first)

            ln_rstd(0, 0)
            ln_low(0, 0)
            ln_rstd(0, 1)
            ffn(0)
            pool.wait_ge(c_out[B - 1], 64)
            stage_content(pool, 0, 0, B - 1, staged_first)
            stage_keys(pool, 0, 0, staged_first)

            def spread_v(h, par):
                for quad in range(4):
                    q = slice(32 * quad, 32 * quad + 32)
                    if not (isinstance(h, int) and h * 4 + quad == 0):
                        pool.wait_ge(v_diag_ready, h * 4 + quad)
                    nc.gpsimd.tensor_copy(v_diag[q, par, :, quad, :],
                                          v_rep[q, :, bass.ds(h * HP, HP)]).then_inc(v_diag_ready, 1)

            pool.wait_ge(v_diag_zero, 1)
            pool.wait_ge(v_rep_in, 16 * 16)
            spread_v(0, 0)
            spread_v(1, 1)
            pool.wait_ge(v_diag_ready, 8)
            for g in range(B):
                part = x[:, 4 * g:4 * g + 4, :]
                nc.gpsimd.tensor_tensor(part, part, rep_ap(bo_row, [(0, 4), (1, D)]), ALU.add)\
                    .then_inc(x_bo, 1)
            pool.wait_ge(x_bo, B)
            with pool.Fori(0, (H - 2) // 2) as it:
                for k in range(2):
                    pool.wait_ge(av_ready, it * 2 + (k + 1))
                    spread_v(it * 2 + (2 + k), k)
            pool.wait_ge(v_diag_ready, 4 * H)
            ln_rstd(2, 0)
            ln_rstd(2, 1)
            ln_low(2, 0)
            ffn(1)

        @block.scalar
        def _(act):
            act.dma_start(pTf[:, 14336:15360], w12_d).then_inc(w_in, 16)
            act.dma_start(ident[:, :], ident_d).then_inc(ident_in, 16)
            act.dma_start(vectors[:, :], vectors_d).then_inc(vectors_in, 16)
            act.dma_start(rows[:, :, :].rearrange("p a n -> p (a n)"),
                          bass.AP(rows_d.tensor, rows_d.offset, [[0, 128], [1, 3 * D]])).then_inc(rows_in, 16)

            def ln_evac(f, g):
                s = ln[f]
                act.wait_ge(s["turned"], 4 * g + 4)
                c = slice(g * 512, (g + 1) * 512)
                src = ps[ln_bank(f, g)]
                if f == 1:
                    nc.scalar.activation(xT[:, c], src, ACT.Copy).then_inc(s["xT"], 1)
                else:
                    nc.scalar.activation(xT_high[:, c], src, ACT.Identity, scale=g1c, bias=lb1c)\
                        .then_inc(s["xT"], 1)
                    nc.scalar.activation(xT[:, c], src, ACT.Identity, scale=g1c, bias=lb1c)\
                        .then_inc(s["xT"], 1)

            def q_high_halves(b):
                if b == 0:
                    act.wait_ge(bias_cols_ready, 2)
                act.wait_ge(q_mm, b + 1)
                for n, (hi, bias) in enumerate(((vh[:, b, 0:S], qvc), (uh[:, b * S:(b + 1) * S], quc))):
                    dst, src = by_row(1 - n, hi, ps[0])
                    nc.scalar.activation(dst, src, ACT.Identity, bias=bias).then_inc(q_high, 1)

            def k_high_half(b):
                act.wait_ge(k_mm, b + 1)
                nc.scalar.activation(kh[:, b * S:(b + 1) * S], ps[1], ACT.Identity, bias=bkc).then_inc(k_high, 1)

            def ffn(f):
                s = ff[f]
                for n in range(STEPS[f]):
                    g, c = divmod(n, HC)
                    if n < NT:
                        act.wait_ge(s["hid"], n + 1)
                        if g >= 2:
                            act.wait_ge(s["ffn"], 4 * (g - 1))
                        nc.scalar.activation(ge[:, n % 8, :], ps[n % 2], ACT.Gelu, scale=wstep[:, 0:1],
                                             bias=b1c[:, c:c + 1]).then_inc(s["gelu"], 1)
                    if n in TURN_STEPS:
                        ln_evac(2 * f, TURN_STEPS[n])
                    m = n - 1
                    if 0 <= m < NT:
                        act.wait_ge(s["gelu"], m + 1)
                        if m == 0 and f == 0:
                            act.wait_ge(pivot_ready, 1)
                        if m >= 2:
                            act.wait_ge(s["sq_summed"], sums(m - 2))
                        nc.scalar.activation(sq[:, m % 2, :], ge[:, m % 8, :], ACT.Square,
                                             bias=minus_pivot).then_inc(s["squared"], 1)
                    if f == 1:
                        continue
                    if n == 7:
                        act.wait_ge(pos_mm, 1)
                        nc.scalar.activation(pf, ps[5], ACT.Identity, bias=bpc).then_inc(pos_f, 1)
                    if n in TURN1_STEPS:
                        ln_evac(1, TURN1_STEPS[n])
                    if n - 1 in QK_STEPS:
                        q_high_halves(QK_STEPS[n - 1])
                        k_high_half(QK_STEPS[n - 1])

            act.wait_ge(vectors_in, 16)
            nc.scalar.activation(gelu_b1, b1c, ACT.Gelu).then_inc(gelu_b1_ready, 1)
            ln_evac(0, 0)
            act.wait_ge(tern_turned, 1)
            nc.scalar.activation(w1T[:, :], ps[0], ACT.Copy).then_inc(w1_ready, 1)
            ffn(0)

            def exp_tile(h, q):
                if q % 2 == 0:
                    act.wait_ge(max_ready, h * NP + (q // 2 + 1))
                    if not (isinstance(h, int) and h * NQ + q < 4):
                        act.wait_ge(pT_ready, h * NP + (q // 2 - 1))
                nc.scalar.activation(probs[:, q % 4, :], ps[q % 4], ACT.Exp,
                                     bias=negmax[:, q % 8:q % 8 + 1],
                                     accum_out=rowsum[:, bass.ds(h * NQ + q, 1)]).then_inc(probs_ready, 1)

            def take_o(h, par, pair):
                act.wait_ge(av_ready, h + 1)
                if not (isinstance(h, int) and h < 2):
                    act.wait_ge(o_out[par], pair * 16)
                nc.scalar.activation(o_sb[:, par, :], ps[4 + par][:, 0:128], ACT.Copy).then_inc(o_ready, 1)

            for h in range(2):
                for q in range(NQ):
                    exp_tile(h, q)
            for h in range(2, 4):
                for q in range(NQ):
                    exp_tile(h, q)
                    if q == 3:
                        take_o(h - 2, h % 2, 0)
            with act.Fori(0, (H - 4) // 2) as it:
                for k in range(2):
                    for q in range(NQ):
                        exp_tile(it * 2 + (4 + k), q)
                        if q == 3:
                            take_o(it * 2 + (2 + k), k, it + 1)
            for h in (H - 2, H - 1):
                take_o(h, h % 2, H // 2 - 1)
            ln_evac(2, 0)
            ffn(1)

        @block.vector
        def _(dve):
            steps = [0]

            def chain(ins):
                ins.then_inc(dve_step, 1)
                steps[0] += 1
                dve.wait_ge(dve_step, steps[0])

            def ln_stats(f, g):
                s = ln[f]
                for t in range(4 * g, 4 * g + 5):
                    if t < 4 * g + 4:
                        x_made(dve, f, t)
                        if t > 1:
                            dve.wait_ge(s["mean"], t - 1)
                        nc.vector.bn_stats(stat[:, t % 2, :], x[:, t, :]).then_inc(s["stat"], 1)
                    if t > 4 * g:
                        dve.wait_ge(s["stat"], t)
                        nc.vector.bn_aggr(mv[:, t - 1, :], stat[:, (t - 1) % 2, :]).then_inc(s["mean"], 1)

            def ln_xhat(f, t):
                s = ln[f]
                dve.wait_ge(s["rstd"], t // 4 + 1)
                if t >= 4:
                    dve.wait_ge(s["turned"], t - 3)
                nc.vector.tensor_scalar(xh[:, t % 4, :], x[:, t, :], mv[:, t, 0:1], rs[:, t:t + 1],
                                        ALU.subtract, ALU.mult).then_inc(s["xhat"], 1)

            def ln_xhats(f, g):
                for t in range(4 * g, 4 * g + 4):
                    ln_xhat(f, t)

            def ternary(n, w):
                sc = wscale[:, n:n + 1]
                nc.vector.tensor_scalar(tmp_t[:, 0, :], w, sc, 0.5, ALU.mult, ALU.is_gt)
                chain(nc.vector.tensor_scalar(tmp_t[:, 1, :], w, sc, -0.5, ALU.mult, ALU.is_lt))
                nc.vector.tensor_tensor(tern[:, n, :], tmp_t[:, 0, :], tmp_t[:, 1, :], ALU.subtract)\
                    .then_inc(tern_ready, 1)
                dve.wait_ge(tern_ready, n + 1)

            ln_stats(0, 0)
            dve.wait_ge(w_in, 16)
            nc.vector.tensor_reduce(wsum[:, 0:1], w1_sb, AX.XY, ALU.add,
                                    apply_absolute_value=True)
            nc.vector.tensor_reduce(wsum[:, 1:2], w2_sb, AX.X, ALU.add,
                                    apply_absolute_value=True).then_inc(wsum_ready, 1)
            ln_xhats(0, 0)
            dve.wait_ge(wtotal_ready, 1)
            chain(nc.vector.tensor_scalar(wclip, ps[2][:, 0:2], 1.0 / (D * HID), 1e-5, ALU.mult, ALU.max))
            chain(nc.vector.reciprocal(wscale, wclip))
            nc.vector.reciprocal(wstep, wscale).then_inc(step_ready, 1)
            ternary(0, w1_sb.rearrange("p c n -> p (c n)"))
            ln_stats(0, 1)
            ternary(1, w2_sb)
            dve.wait_ge(step_ready, 1)
            nc.vector.tensor_scalar(half_step, wstep[:, 1:2], 0.5, None, ALU.mult).then_inc(half_step_ready, 1)
            ln_xhats(0, 1)
            dve.wait_ge(pivot_summed, 1)
            chain(nc.vector.tensor_reduce(pivot_sum, ps[5][:, 0:HC], AX.X, ALU.add, negate=True))
            nc.vector.tensor_scalar(minus_pivot, pivot_sum, 1.0 / HID, None, ALU.mult).then_inc(pivot_ready, 1)
            dve.wait_ge(vectors_in, 16)
            dve.wait_ge(tern_turned, 2)
            dve.wait_ge(half_step_ready, 1)
            for dst, v, done in ((w2g, g2c, w2g_ready), (w2b, lb2c, w2b_ready)):
                nc.vector.scalar_tensor_tensor(dst, ps[3].rearrange("p (c n) -> p c n", c=HC), half_step,
                                               rep_ap(v, [(1, HC), (0, D)]), ALU.mult, ALU.mult)\
                    .then_inc(done, 1)
            ln_stats(0, 2)
            def centre_w2():
                dve.wait_ge(w2g_ready, 1)
                dve.wait_ge(w2_summed, 1)
                nc.vector.scalar_tensor_tensor(w2c[:, :, 0:D], rep_ap(ps[4][:, 0:D], [(0, HC), (1, D)]),
                                               -1.0 / HID, w2g, ALU.mult, ALU.add).then_inc(w2_ready, 1)
                dve.wait_ge(rows_in, 16)
                dve.wait_ge(const_summed, 1)
                nc.vector.scalar_tensor_tensor(half_const[:, :], b2_row, 0.5, ps[2][:, 0:D],
                                               ALU.mult, ALU.add).then_inc(const_ready, 1)

            def split_positions():
                dve.wait_ge(pos_f, 1)
                dve.wait_ge(zs_zero, 1)
                chain(nc.vector.tensor_copy(zs[:, 0, 0:S], pf))
                nc.vector.tensor_copy(zs[:, 2, S + 1:2 * S], zs[:, 0, 0:S - 1]).then_inc(pos_split, 1)
                chain(nc.vector.tensor_tensor(zs[:, 1, 0:S], pf, zs[:, 0, 0:S], ALU.subtract))
                nc.vector.tensor_copy(zs[:, 3, S + 1:2 * S], zs[:, 1, 0:S - 1]).then_inc(pos_split, 1)

            def query_biases():
                for dst, src in ((quc, uc), (qvc, vc)):
                    chain(nc.vector.tensor_tensor(dst, bqc, src, ALU.add))
                    nc.vector.tensor_scalar(dst, dst, SCALE, None, ALU.mult).then_inc(bias_cols_ready, 1)
                dve.wait_ge(qkv_weights_in, 16)
                nc.vector.tensor_scalar(wq_s, wq_sb, SCALE, None, ALU.mult).then_inc(wq_scaled, 1)

            def add_attention(b):
                dve.wait_ge(wo_mm, b + 1)
                dve.wait_ge(x_bo, B)
                nc.vector.tensor_tensor(x[:, 4 * b:4 * b + 4, :], x[:, 4 * b:4 * b + 4, :],
                                        ps[4 + b % 2].rearrange("p (t n) -> p t n", t=4), ALU.add)\
                    .then_inc(x_attn, 1)

            def ffn(f):
                s = ff[f]
                for n in range(STEPS[f]):
                    m = n - 1
                    g, c = divmod(m, HC)
                    if 0 <= m < NT and c:
                        dve.wait_ge(s["squared"], m + 1)
                        if m > 1:
                            dve.wait_ge(s["sq_summed"], sums(m) - 1)
                        if c == 1 and g:
                            dve.wait_ge(s["sq_split"], 2 * g)
                        nc.vector.tensor_tensor(sqsum, sq[:, 0, :] if c == 1 else sqsum, sq[:, m % 2, :],
                                                ALU.add).then_inc(s["sq_summed"], 1)
                    if 0 <= m < NT and c == HC - 1:
                        dve.wait_ge(s["sq_summed"], sums(m))
                        if g:
                            dve.wait_ge(s["sq_mean"], g)
                        nc.vector.tensor_copy(sq_high, sqsum).then_inc(s["sq_split"], 1)
                        dve.wait_ge(s["sq_split"], 2 * g + 1)
                        nc.vector.tensor_tensor(sq_low, sqsum, sq_high, ALU.subtract).then_inc(s["sq_split"], 1)
                    g = (n - 9) // 4
                    if n % 4 == 1 and 0 <= g < B:
                        cols4 = slice(4 * g, 4 * g + 4)
                        dve.wait_ge(s["ffn"], 4 * g + 4)
                        dve.wait_ge(s["sq_mean"], g + 1)
                        mean = moments(g)[:, :, 0:2 * (D + 1)].rearrange("p a (t n) -> p a t n", t=2)[:, :, :, D]
                        nc.vector.tensor_scalar(gmean[:, cols4].rearrange("p (a t) -> p a t", a=2), mean,
                                                minus_pivot, None, ALU.add).then_inc(s["gmean"], 1)
                        dve.wait_ge(s["gmean"], g + 1)
                        nc.vector.tensor_tensor(gmean[:, cols4], gmean[:, cols4], gmean[:, cols4], ALU.mult)\
                            .then_inc(s["gmean_sq"], 1)
                        dve.wait_ge(s["gmean_sq"], g + 1)
                        nc.vector.tensor_tensor(gvar[:, cols4], moments(g)[:, 0, SQ0:SQ0 + 4], gmean[:, cols4],
                                                ALU.subtract).then_inc(s["gvar"], 1)
                    g = (n - 10) // 4
                    if n % 4 == 2 and 0 <= g < B:
                        dve.wait_ge(s["grstd"], g + 1)
                        dve.wait_ge(s["x_const"], g + 1)
                        for t in range(4 * g, 4 * g + 4):
                            nc.vector.scalar_tensor_tensor(x[:, t, :], out_tile(t)[:, 0:D], grs[:, t:t + 1],
                                                           x[:, t, :], ALU.mult, ALU.add).then_inc(s["x_new"], 1)
                    if n == 3 and f == 0:
                        centre_w2()
                    if n in (4, 6):
                        ln_xhats(2 * f, n // 2)
                    if n == 4:
                        if f == 1:
                            add_attention(3)
                        ln_stats(2 * f, 3)
                    if f == 1:
                        continue
                    if n == 8:
                        split_positions()
                    if n == 11:
                        query_biases()
                    if n % 4 == 2 and 0 <= (n - 10) // 4 < B:
                        ln_stats(1, (n - 10) // 4)
                    if n in XHAT1_STEPS:
                        ln_xhats(1, XHAT1_STEPS[n])
                    if n - 1 in QK_STEPS:
                        q_low_halves(QK_STEPS[n - 1])
                        k_low_half(QK_STEPS[n - 1])
                    if n - 2 in QK_STEPS:
                        v_bias(QK_STEPS[n - 2])

            def q_low_halves(b):
                c = slice(b * S, (b + 1) * S)
                dve.wait_ge(q_high, 2 * b + 2)
                for n, (hi, lo, bias) in enumerate(((vh[:, b, 0:S], vl[:, b, 0:S], qvc), (uh[:, c], ul[:, c], quc))):
                    dst, src = by_row(1 - n, lo, ps[0])
                    high = by_row(1 - n, hi, ps[0])[0]
                    for j in range(4 if n else 1):
                        part = (slice(None), j) if n else (slice(None),)
                        ins = nc.vector.scalar_tensor_tensor(dst[part], src[part], bias, high[part],
                                                             ALU.add, ALU.subtract)
                    ins.then_inc(q_split, 1)
                dve.wait_ge(q_split, 2 * b + 1)
                nc.vector.tensor_copy(vh[:, b, S:VW], vh[:, b, 1:NG + 1])
                nc.vector.tensor_copy(vl[:, b, S:VW], vl[:, b, 1:NG + 1]).then_inc(v_extended, 1)

            def k_low_half(b):
                c = slice(b * S, (b + 1) * S)
                dve.wait_ge(k_high, b + 1)
                nc.vector.scalar_tensor_tensor(kl[:, c], ps[1], bkc, kh[:, c], ALU.add, ALU.subtract)\
                    .then_inc(k_split, 1)

            def v_bias(b):
                dve.wait_ge(v_mm, b + 1)
                nc.vector.tensor_tensor(v_sb[:, 4 * b:4 * b + 4, :], ps[2].rearrange("p (t n) -> p t n", t=4),
                                        rep_ap(bv_row, [(0, 4), (1, D)]), ALU.add).then_inc(v_ready, 1)

            ffn(0)
            for b in range(B):
                dve.wait_ge(c_out[b], 64)
            dve.wait_ge(q_out, 16 * 3 * B)

            def row_max(h, n):
                dve.wait_ge(scores_ready, h * NP + (n + 1))
                nc.vector.tensor_reduce(negmax[:, 2 * n % 8:2 * n % 8 + 2], pairs[n % 2][:, :, :], AX.X,
                                        ALU.max, negate=True).then_inc(max_ready, 1)

            def turn(h, par, n):
                dve.wait_ge(probs_ready, h * NQ + (2 * n + 2))
                if n == 0 and isinstance(h, int) and h == 1:
                    dve.wait_ge(v_rep_in, 16 * 16)
                if n == 0 and not (isinstance(h, int) and h < 2):
                    dve.wait_ge(av_ready, h - 1)
                nc.vector.transpose(pT[:, par, 2 * n:2 * n + 2, :].rearrange("p a s -> p (a s)"),
                                    probs[:, 2 * n % 4:2 * n % 4 + 2, :].rearrange("p a s -> p (a s)"))\
                    .then_inc(pT_ready, 1)

            def head(h, par, first=False):
                for n in range(NP):
                    row_max(h, n)
                    if n >= 1:
                        turn(h, par, n - 1)
                    elif not first:
                        turn(h - 1, 1 - par, NP - 1)

            head(0, 0, True)
            head(1, 1)
            head(2, 0)
            head(3, 1)
            with dve.Fori(0, (H - 4) // 2) as it:
                for k in range(2):
                    head(it * 2 + (4 + k), k)
            turn(H - 1, 1, NP - 1)

            dve.wait_ge(av_ready, H - 1)
            nc.vector.reciprocal(rec, rowsum[:, :]).then_inc(rec_ready, 1)
            dve.wait_ge(rec_ready, 1)
            src = rec.rearrange("p (h q) -> p q h", q=NQ)
            for e in range(HP):
                ins = nc.vector.tensor_copy(recx[:, :, :, e], src)
            ins.then_inc(recx_ready, 1)
            dve.wait_ge(attn_in, 16 * H)
            av = attnT.rearrange("p (b j q i) -> p b q j i", b=B, j=4, q=NQ)
            for b in range(B):
                for n in range(4):
                    dve.wait_ge(rec_turned, n + 1)
                    r = ps[n].rearrange("p (q j b i) -> p b q j i", q=4, j=4, b=B)[:, b]
                    a = av[:, b, 4 * n:4 * n + 4]
                    ins = nc.vector.tensor_tensor(a, a, r, ALU.mult)
                ins.then_inc(attn_scaled, 1)
            for b in range(B - 1):
                add_attention(b)
                ln_stats(2, b)
                if b:
                    ln_xhats(2, b - 1)
            ffn(1)

        @block.tensor
        def _(pe):
            mm = nc.tensor.matmul
            pe.wait_ge(ones_set, 1)
            pe.wait_ge(wsum_ready, 1)
            mm(ps[2][:, 0:2], ones[:, :], wsum, start=True, stop=True).then_inc(wtotal_ready, 1)

            def turn_weights(n, bank):
                pe.wait_ge(tern_ready, n + 1)
                for c in range(HC):
                    ins = nc.tensor.transpose(bank[:, c * 128:(c + 1) * 128],
                                              tern[:, n, c * 128:(c + 1) * 128], ident[:, :])
                ins.then_inc(tern_turned, 1)

            def ln_turn(f, t):
                s = ln[f]
                g = t // 4
                pe.wait_ge(s["xhat"], t + 1)
                if g >= 2:
                    pe.wait_ge(s["xT"], (g - 1) * (1 if f == 1 else 2))
                elif f == 1:
                    pe.wait_ge(ln[0]["xT"], 2 * B)
                nc.tensor.transpose(ps[ln_bank(f, g)][:, (t % 4) * 128:(t % 4 + 1) * 128], xh[:, t % 4, :],
                                    ident[:, :]).then_inc(s["turned"], 1)

            def ffn(f):
                s = ff[f]
                for n in range(STEPS[f]):
                    g, c = divmod(n, HC)
                    if n < NT:
                        pe.wait_ge(ln[2 * f]["xT_low"], g + 1)
                        if n >= 2:
                            pe.wait_ge(s["gelu"], n - 1)
                        k = slice(c * 128, (c + 1) * 128)
                        tokens = slice(g * 512, (g + 1) * 512)
                        mm(ps[n % 2], w1T[:, k], xT_high[:, tokens], start=True, stop=False)
                        mm(ps[n % 2], w1T[:, k], xT_low[:, tokens], start=False, stop=True).then_inc(s["hid"], 1)
                    g = (n - 7) // 4
                    if n % 4 == 3 and 0 <= g < B:
                        pe.wait_ge(s["sq_split"], 2 * g + 2)
                        for t in range(4):
                            k = slice(t * 128, (t + 1) * 128)
                            o = moments(g)[:, 0, SQ0 + t:SQ0 + t + 1]
                            mm(o, sq_high[:, k], mean16[:, :], start=True, stop=False)
                            ins = mm(o, sq_low[:, k], mean16[:, :], start=False, stop=True)
                        ins.then_inc(s["sq_mean"], 1)
                    t = n - 5
                    if 0 <= t < NT:
                        g = t // 4
                        if t == 0 and f == 0:
                            pe.wait_ge(w2_ready, 1)
                            pe.wait_ge(const_ready, 1)
                        if t == 4:
                            if f == 0:
                                pe.wait_ge(pos_f, 1)
                            else:
                                pe.wait_ge(x_attn, B)
                        if t % 4 == 0:
                            pe.wait_ge(s["gelu"], t + 4)
                            if g >= 2:
                                pe.wait_ge(s["x_new"], 4 * (g - 1))
                        k = slice(t % 4 * 128, (t % 4 + 1) * 128)
                        for c in range(HC):
                            ins = mm(out_tile(t), ge[:, (4 * g + c) % 8, k], w2c[:, c, :],
                                     start=(c == 0), stop=(c == HC - 1))
                        ins.then_inc(s["ffn"], 1)
                    if n == 1 and f == 0:
                        turn_weights(1, ps[3])
                    if n in TURN_STEPS:
                        for t in range(4):
                            ln_turn(2 * f, 4 * TURN_STEPS[n] + t)
                    if f == 1:
                        continue
                    if n == 6:
                        pe.wait_ge(pos_weights_in, 16)
                        pe.wait_ge(pivot_ready, 1)
                        mm(ps[5], wp_sb, embT, start=True, stop=True).then_inc(pos_mm, 1)
                    if n == 2:
                        for bank, src, ready, done in ((4, w2g, w2g_ready, w2_summed),
                                                       (2, w2b, w2b_ready, const_summed)):
                            pe.wait_ge(ready, 1)
                            for c in range(HC):
                                ins = mm(ps[bank][:, 0:D], ones[:, :], src[:, c, :], start=(c == 0),
                                         stop=(c == HC - 1))
                            ins.then_inc(done, 1)
                    if n in TURN1_STEPS:
                        for t in range(4):
                            ln_turn(1, 4 * TURN1_STEPS[n] + t)
                    if n in QK_STEPS:
                        q_product(QK_STEPS[n])
                        k_product(QK_STEPS[n])
                    if n - 1 in QK_STEPS:
                        v_product(QK_STEPS[n - 1])

            def q_product(b):
                pe.wait_ge(ln[1]["xT"], b + 1)
                if b == 0:
                    pe.wait_ge(wq_scaled, 1)
                    pe.wait_ge(qkv_weights_in, 16)
                    pe.wait_ge(ff[0]["gelu"], NT)
                else:
                    pe.wait_ge(q_split, 2 * b)
                mm(ps[0], wq_s, xT[:, b * S:(b + 1) * S], start=True, stop=True).then_inc(q_mm, 1)

            def k_product(b):
                if b:
                    pe.wait_ge(k_split, b)
                mm(ps[1], wk_sb, xT[:, b * S:(b + 1) * S], start=True, stop=True).then_inc(k_mm, 1)

            def v_product(b):
                if b:
                    pe.wait_ge(v_ready, b)
                else:
                    pe.wait_ge(ff[0]["x_new"], 3 * 4)
                for t in range(4):
                    c = slice(b * S + t * 128, b * S + (t + 1) * 128)
                    ins = mm(ps[2][:, t * 128:(t + 1) * 128], xT[:, c], wv_sb, start=True, stop=True)
                ins.then_inc(v_mm, 1)

            pe.wait_ge(ident_in, 16)
            for t in range(4):
                ln_turn(0, t)
            turn_weights(0, ps[0])
            pe.wait_ge(gelu_b1_ready, 1)
            mm(ps[5][:, 0:HC], ones[:, :], gelu_b1, start=True, stop=True).then_inc(pivot_summed, 1)
            pe.wait_ge(w1_ready, 1)
            ffn(0)
            pe.wait_ge(v_ready, B)

            def scores(h, par, q):
                if not (isinstance(h, int) and h * NQ + q < 4):
                    pe.wait_ge(probs_ready, h * NQ + (q - 3))
                bank = ps[q % 4]

                def rows(a, j):
                    return a.rearrange("k (b g) -> k b g", g=NG)[:, :, j * NQ + q]

                all_rows = stage_c[:, par, :].rearrange("k (m g) -> k m g", g=NQ)[:, :, q]
                mm(bank, all_rows, stage_k[:, par, :], start=True, stop=False, skip_group_check=True)
                for j in range(4):
                    a0 = 128 * j + NI * q
                    o = bank[32 * j:32 * j + 32, :]
                    m0 = S - NI - a0
                    mm(o, rows(stage_q[:, par, 0, :], j), stage_z[:, par, 0, m0:m0 + S], start=False,
                       stop=False, skip_group_check=True)
                for j in range(4):
                    a0 = 128 * j + NI * q
                    n = a0 + NI
                    m0 = S - NI - a0
                    mm(bank[32 * j:32 * j + 32, 0:n], rows(stage_q[:, par, 1, :], j),
                       stage_z[:, par, 1, m0:m0 + n], start=False, stop=False, skip_group_check=True)
                for j in range(4):
                    a0 = 128 * j + NI * q
                    m0 = S - NI - a0
                    ins = mm(bank[32 * j:32 * j + 32, a0 + 2:S], rows(stage_q[:, par, 2, :], j),
                             stage_z[:, par, 2, m0 + a0 + 2:m0 + S], start=False, stop=True,
                             skip_group_check=True)
                if q % 2:
                    ins.then_inc(scores_ready, 1)

            def values(h, par, kb):
                if kb == 0:
                    pe.wait_ge(pT_ready, (h + 1) * NP)
                    pe.wait_ge(v_diag_ready, (h + 1) * 4)
                    if not (isinstance(h, int) and h < 2):
                        pe.wait_ge(o_ready, h - 1)
                for b in range(B):
                    mov = pT[:, par, :, 32 * kb + NI * b:32 * kb + NI * (b + 1)]
                    ins = mm(ps[4 + par][32 * b:32 * b + 32, 0:128],
                             v_diag[:, par, b * KB + kb, :, :].rearrange("p j e -> p (j e)"), mov,
                             start=(kb == 0), stop=(kb == KB - 1), skip_group_check=True)
                if kb == KB - 1:
                    ins.then_inc(av_ready, 1)

            LAG = 4

            def head(h, par, staged_count, first=False):
                pe.wait_ge(staged[par], staged_count)
                for q in range(NQ):
                    scores(h, par, q)
                    if not first and q >= LAG:
                        values(h - 1, 1 - par, q - LAG)
                if not first:
                    for kb in range(NQ - LAG, KB):
                        values(h - 1, 1 - par, kb)

            pe.wait_ge(staged_first, 16 * LOADS_FIRST)
            head(0, 0, 16 * (LOADS - LOADS_FIRST), True)
            head(1, 1, 16 * LOADS)
            head(2, 0, 16 * (2 * LOADS - LOADS_FIRST))
            with pe.Fori(0, (H - 4) // 2) as it:
                for k in range(2):
                    head(it * 2 + (3 + k), 1 - k, (it + (2 + k)) * (16 * LOADS) - 16 * LOADS_FIRST * k)
            head(H - 1, 1, (H // 2) * 16 * LOADS)
            for kb in range(KB):
                values(H - 1, 1, kb)
                if kb < KB - 4:
                    continue
                if kb == KB - 4:
                    pe.wait_ge(recx_ready, 1)
                n = kb - (KB - 4)
                for q in range(4 * n, 4 * n + 4):
                    ins = mm(ps[n][:, (q % 4) * 128:(q % 4 + 1) * 128],
                             recx[:, q, :, :].rearrange("p h e -> p (h e)"), ident[:, :], start=True, stop=True)
                ins.then_inc(rec_turned, 1)
            pe.wait_ge(o_ready, H)
            pe.wait_ge(wo_in, 16)
            for b in range(B):
                pe.wait_ge(attn_scaled, b + 1)
                if b >= 2:
                    pe.wait_ge(x_attn, b - 1)
                for t in range(4):
                    ins = mm(ps[4 + b % 2][:, t * 128:(t + 1) * 128],
                             attnT[:, b * S + t * 128:b * S + (t + 1) * 128], wo_sb[:, :],
                             start=True, stop=True)
                ins.then_inc(wo_mm, 1)
                if b == 2:
                    for t in range(4):
                        ln_turn(2, t)
            ffn(1)


def kernel(**inputs):
    import concourse.bacc as bacc
    from concourse.bass_utils import run_bass_kernel_spmd

    pos = np.arange(S, dtype=np.float32)
    idx = np.arange(D // 2, dtype=np.float32)
    inv_freq = (np.float32(1.0) / np.float32(10000.0) ** (np.float32(2.0) * idx / np.float32(D))).astype(np.float32)
    ang = pos[:, None] * inv_freq[None, :]
    emb = np.concatenate([np.sin(ang), np.cos(ang)], axis=-1).astype(np.float32)

    nc = bacc.Bacc("TRN2", target_bir_lowering=False, num_devices=1)
    a = {n: np.asarray(v) for n, v in inputs.items()}
    at = {n[3:]: v for n, v in a.items()}
    vectors = [at[n].reshape(-1) for n in ("ffn_ln1_g", "ffn_ln1_b", "attn_bq", "attn_u", "attn_v", "attn_bk",
                                           "attn_bp", "ffn_ln2_g", "ffn_ln2_b", "ffn_b1")]
    laid_out = [
        ("x", at["attn_x"]),
        ("w12", np.concatenate([at["ffn_w1"].reshape(HC, 128, D).transpose(1, 0, 2).reshape(128, HID),
                                at["ffn_w2"]], axis=1)),
        ("vectors", np.concatenate(vectors).reshape(-1, 128).T),
        ("rows", np.concatenate([at["ffn_b2"], at["attn_bo"], at["attn_bv"]])),
        ("wqkv", np.concatenate([at["attn_Wq"], at["attn_Wk"], at["attn_Wv"]], axis=1)),
        ("wo", at["attn_Wo"]),
        ("wp_emb", np.concatenate([at["attn_Wp"], emb.T], axis=1)),
        ("ident", np.eye(128, dtype=np.float32)),
    ]
    arrays, args = {}, []
    for name, value in laid_out:
        value = np.ascontiguousarray(value)
        arrays[f"in_{name}"] = value
        args.append(nc.dram_tensor(f"in_{name}", value.shape, mybir.dt.from_np(value.dtype),
                                   kind="ExternalInput").ap())
    out = nc.dram_tensor("out_0", (B, S, D), F32, kind="ExternalOutput").ap()
    macaron_kernel(nc, args, out)
    r = run_bass_kernel_spmd(nc, [arrays], core_ids=[0])
    return r.results[0]["out_0"]
```

```python
from contextlib import ExitStack

import numpy as np

import concourse.bass as bass
from concourse import mybir

F32 = mybir.dt.float32
F16 = mybir.dt.float16
U32 = mybir.dt.uint32
ALU = mybir.AluOpType
ACT = mybir.ActivationFunctionType
AX = mybir.AxisListType

B, S, D = 4, 512, 128
H, HP = 16, 8
HID = 512
NT = B * S // 128
HC = HID // 128
NI = 8
NQ = S // 4 // NI
NG = S // NI
KB = S // 32
EPS = 1e-5
SCALE = float(HP) ** -0.5
NP = NQ // 2
ZW = 2 * S - NI
ZB0 = S - NI + 2
STEPS = (27, 22)
TURN_STEPS = ({1: 1, 4: 2, 8: 3}, {0: 1, 3: 2, 6: 3})
XHAT1_STEPS = {12: 0, 16: 1, 19: 2, 22: 3}
TURN1_STEPS = {14: 0, 18: 1, 20: 2, 23: 3}
QK_STEPS = {17: 0, 20: 1, 22: 2, 24: 3}
QK_BANKS = ((0, 1), (0, 1), (4, 5), (0, 1))
VW = S + S // NI
LOADS = 16
LOADS_FIRST = 6


def macaron_kernel(nc, ins, out):
    x_d, w12_d, vectors_d, rows_d, wqkv_d, wo_d, wp_emb_d, ident_d = ins

    qs_dram = nc.dram_tensor("qs_scratch", (D, 2, 3, B * S), F16, kind="Internal").ap()
    qc_dram = nc.dram_tensor("qc_scratch", (D, 4, B * S), F16, kind="Internal").ap()
    kc_dram = nc.dram_tensor("kc_scratch", (D, 4, B, S), F16, kind="Internal").ap()
    z_dram = nc.dram_tensor("z_scratch", (D, 2, 3, 2 * S), F16, kind="Internal").ap()
    at_dram = nc.dram_tensor("attn_scratch", (H, HP, 16, 128), F32, kind="Internal").ap()

    with ExitStack() as ctx:
        def sb(name, shape, dt=F32):
            return ctx.enter_context(nc.sbuf_tensor(name, shape, dt))

        def sem(name):
            return ctx.enter_context(nc.semaphore(name))

        x = sb("x", [128, NT, D])
        xT = sb("xT", [128, B * S])
        xh = sb("xh", [128, 4, D])
        ident = sb("ident", [128, 128])
        ones = sb("ones", [128, 128])
        w1T = sb("w1T", [128, HID], F16)
        w2c = sb("w2c", [128, HC, D + 1])
        mean16 = sb("mean16", [128, 1], F16)
        half_const = sb("half_const", [128, D])
        rows = sb("rows", [128, 3, D])
        wo_sb = sb("wo_sb", [128, D])
        vectors = sb("vectors", [128, 19])
        cols = sb("cols", [128, 32])
        minus_half = sb("minus_half", [128, 8])
        stat = sb("stat", [128, 4, 6])
        mv = sb("mv", [128, NT, 2])
        rs = sb("rs", [128, NT])
        gmean = sb("gmean", [128, NT])
        gvar = sb("gvar", [128, NT])
        grs = sb("grs", [128, NT])
        stage_q = sb("stage_q", [128, 2, 3, B * S], F16)
        stage_c = sb("stage_c", [128, 2, B * S], F16)
        stage_k = sb("stage_k", [128, 2, S], F16)
        stage_z = sb("stage_z", [128, 2, 3, ZW], F16)
        probs = sb("probs", [128, 6, S])
        negmax = sb("negmax", [128, 8])
        rowsum = sb("rowsum", [128, H * NQ])
        pT = sb("pT", [128, 2, NQ, S])
        v_rep = sb("v_rep", [128, B * KB, D])
        v_diag = sb("v_diag", [128, 2, B * KB, 4, HP])
        sqsum = sb("sqsum", [128, 512])
        o_sb = sb("o_sb", [128, 2, 128])
        pairs = [ctx.enter_context(nc.psum_tensor(f"pair{i}", [128, 2, 512], F32)) for i in range(4)]
        ps = [pairs[i // 2][:, i % 2, :] for i in range(8)]

        pTf = pT[:, :, :, :].rearrange("p a q s -> p (a q s)")
        wq_sb, wk_sb, wv_sb, wp_sb = (pTf[:, 128 * n:128 * n + 128] for n in range(4))
        embT = pTf[:, 512:1024]
        wq_s = pTf[:, 2048:2176]
        w2g = pTf[:, 2176:2688].rearrange("p (c n) -> p c n", c=HC)
        w2b = pTf[:, 2688:3200].rearrange("p (c n) -> p c n", c=HC)
        pf = pTf[:, 3584:4096]
        half = pTf[:, 4096:8192].bitcast(F16).rearrange("p (a n) -> p a n", a=4)
        uh, ul, kh, kl = (half[:, n, :] for n in range(4))
        vl = pTf[:, 8192:8192 + B * VW // 2].bitcast(F16).rearrange("p (b n) -> p b n", b=B)
        vh = pTf[:, 14336:14336 + B * VW // 2].bitcast(F16).rearrange("p (b n) -> p b n", b=B)
        k_full = pTf[:, 9344:9344 + S]
        zs = pTf[:, 10240:12288].bitcast(F16).rearrange("p (a n) -> p a n", a=4)
        v_sb = pTf[:, 12288:14336].rearrange("p (t n) -> p t n", t=NT)
        w1_sb = pTf[:, 14336:14848].rearrange("p (c n) -> p c n", c=HC)
        w2_sb = pTf[:, 14848:15360]
        tern = pTf[:, 15360:16384].rearrange("p (a n) -> p a n", a=2)
        tmp_t = pTf[:, 4096:5120].rearrange("p (a n) -> p a n", a=2)
        vrf = v_rep[:, :, :].rearrange("p a n -> p (a n)")
        xT_high, xT_low = (vrf[:, n:n + 1024].bitcast(F16) for n in (0, 1024))
        ge = vrf[:, 2048:6144].rearrange("p (a n) -> p a n", a=8)
        sq = vrf[:, 6144:7680].rearrange("p (a n) -> p a n", a=3)
        sq_high, sq_low = (vrf[:, n:n + 256].bitcast(F16) for n in (7680, 7936))
        attnT = xT[:, :]
        rec = pTf[:, 2048:2304]
        rec_tokens = pTf[:, 2560:3584].rearrange("p (a n) -> p a n", a=2)
        recx = pTf[:, 4096:6144].rearrange("p (q h e) -> p q h e", q=NQ, h=H)

        g1c, lb1c, bqc, uc, vc, bkc, bpc = (vectors[:, n:n + 1] for n in range(7))
        g2c, lb2c, b1c = (vectors[:, n:n + HC] for n in (7, 11, 15))
        b2_row, bo_row, bv_row = (rows[:, n, :] for n in range(3))
        quc, qvc = cols[:, 0:1], cols[:, 1:2]
        wsum, wclip, wscale, wstep = (cols[:, n:n + 2] for n in (2, 4, 6, 8))
        half_step = cols[:, 10:11]
        gelu_b1 = cols[:, 12:12 + HC]
        pivot_sum = cols[:, 16:17]
        minus_pivot = cols[:, 17:18]

        x_in = [sem(f"x_in{b}") for b in range(B)]
        w_in = sem("w_in")
        vectors_in = sem("vectors_in")
        rows_in = sem("rows_in")
        pos_weights_in = sem("pos_weights_in")
        ident_in = sem("ident_in")
        qkv_weights_in = sem("qkv_weights_in")
        wo_in = sem("wo_in")
        step_ready = sem("step_ready")
        half_step_ready = sem("half_step_ready")
        gelu_b1_ready = sem("gelu_b1_ready")
        pivot_summed = sem("pivot_summed")
        pivot_ready = sem("pivot_ready")
        wq_scaled = sem("wq_scaled")
        ones_set = sem("ones_set")
        wsum_ready = sem("wsum_ready")
        wtotal_ready = sem("wtotal_ready")
        dve_step = sem("dve_step")
        tern_ready = sem("tern_ready")
        tern_turned = sem("tern_turned")
        w1_ready = sem("w1_ready")
        w2g_ready = sem("w2g_ready")
        w2b_ready = sem("w2b_ready")
        w2_summed = sem("w2_summed")
        w2_ready = sem("w2_ready")
        const_summed = sem("const_summed")
        const_ready = sem("const_ready")
        bias_cols_ready = sem("bias_cols_ready")
        stage_zero = sem("stage_zero")
        ln = [{n: sem(f"{n}{f}") for n in ("stat", "mean", "rstd0_", "rstd", "xhat", "turned", "xT", "xT_low")}
              for f in range(3)]
        ff = [{n: sem(f"{n}{f}") for n in ("hid", "gelu", "squared", "sq_summed", "sq_split", "sq_mean",
                                          "gmean", "gmean_sq", "gvar", "gvar_eps", "grstd", "ffn",
                                          "x_const", "x_new")}
              for f in range(2)]
        pos_mm = sem("pos_mm")
        pos_f = sem("pos_f")
        pos_split = sem("pos_split")
        zs_zero = sem("zs_zero")
        q_mm = sem("q_mm")
        k_mm = sem("k_mm")
        v_mm = sem("v_mm")
        q_high = sem("q_high")
        q_split = sem("q_split")
        v_extended = sem("v_extended")
        k_high = sem("k_high")
        k_split = sem("k_split")
        k_split_last = sem("k_split_last")
        v_ready = sem("v_ready")
        v_rep_in = sem("v_rep_in")
        z_out = sem("z_out")
        u_out = [sem(f"u_out{b}") for b in range(B)]
        k_out = sem("k_out")
        q_out = sem("q_out")
        staged = [sem("staged_even"), sem("staged_odd")]
        staged_first = sem("staged_first")
        v_diag_ready = sem("v_diag_ready")
        v_diag_zero = sem("v_diag_zero")
        scores_ready = sem("scores_ready")
        max_ready = sem("max_ready")
        probs_ready = sem("probs_ready")
        pT_ready = sem("pT_ready")
        av_ready = sem("av_ready")
        o_ready = sem("o_ready")
        o_out = [sem("o_out_even"), sem("o_out_odd")]
        attn_in = sem("attn_in")
        rec_ready = sem("rec_ready")
        recx_ready = sem("recx_ready")
        rec_turned = sem("rec_turned")
        rec_out = sem("rec_out")
        attn_scaled = sem("attn_scaled")
        attn_scaled_odd = sem("attn_scaled_odd")
        wo_mm = sem("wo_mm")
        x_bo = sem("x_bo")
        x_attn = sem("x_attn")
        out_done = sem("out_done")

        def x_made(eng, f, t):
            if f == 0:
                eng.wait_ge(x_in[t // 4], 16)
            elif f == 1:
                eng.wait_ge(ff[0]["x_new"], t + 1)
            else:
                eng.wait_ge(x_attn, t // 4 + 1)

        block = ctx.enter_context(nc.Block())

        def sums(m):
            g, c = divmod(m, HC)
            return (HC - 1) * g + max(c, 1)

        def moments(g):
            return pairs[1 + g % 2]

        def out_tile(t):
            return moments(t // 4)[:, t % 4 // 2, t % 2 * (D + 1):(t % 2 + 1) * (D + 1)]

        def score_pair(n):
            return pairs[(0, 1, 3)[n % 3]]

        def slot_before(h, n):
            return h * NP + (n - 2) if n >= 3 else h * NP + ((6, 7, 5)[n] + 1 - NP)

        SQ0 = 2 * (D + 1) + 2

        def ln_bank(f, g):
            return 6 + g % 2

        def by_row(n, dst, src):
            if n == 0:
                return (dst.rearrange("p (j i g) -> p j i g", j=4, i=NI),
                        src.rearrange("p (j g i) -> p j i g", j=4, i=NI))
            return dst.rearrange("p (i g) -> p i g", i=NI), src.rearrange("p (g i) -> p i g", i=NI)

        def stage_content(eng, h, par, b, done):
            c_rows = qc_dram.rearrange("(h p) t n -> h (p t) n", p=HP)[h]
            dst = stage_c[32 * b:32 * b + 32, par, :].rearrange("r (j b m) -> r j b m", j=4, b=B)[:, :, b]
            src = c_rows[:, b * S:(b + 1) * S].rearrange("r (j m) -> r j m", j=4)
            eng.dma_start(dst, src).then_inc(done, 16)

        def stage_keys(eng, h, par, done):
            k_rows = kc_dram.rearrange("(h p) t b n -> h b (p t) n", p=HP)[h]
            eng.dma_start(stage_k[:, par, :], k_rows).then_inc(done, 16)

        def stage_queries(eng, h, par, done, rows_i=range(NI)):
            q_rows = qs_dram.rearrange("(h p) t k n -> h (p t) k n", p=HP)[h]
            for ii in rows_i:
                i = NI - 1 - ii
                src = q_rows.rearrange("r k (b m) -> r (k b) m", b=B)[:, :, i * NG:(i + 1) * NG]
                dst = stage_q[16 * ii:16 * ii + 16, par, :, :].rearrange(
                    "r k (b m) -> r (k b) m", b=B)[:, :, i * NG:(i + 1) * NG]
                eng.dma_start(dst, src).then_inc(done, 16)

        def rep_ap(view, dims):
            return bass.AP(view.tensor, view.offset, [list(view.ap[0])] + [list(d) for d in dims])

        @block.sync
        def _(sp):
            xv = x_d.rearrange("b (t p) d -> b p t d", p=128)
            for b in range(B):
                sp.dma_start(x[:, 4 * b:4 * b + 4, :], xv[b]).then_inc(x_in[b], 16)
            sp.dma_start(pTf[:, 384:1024], wp_emb_d).then_inc(pos_weights_in, 16)
            sp.dma_start(pTf[:, 0:384], wqkv_d).then_inc(qkv_weights_in, 16)
            sp.dma_start(wo_sb[:, :], wo_d).then_inc(wo_in, 16)
            sp.wait_ge(pos_split, 2)
            for t, kind, src in ((0, 0, 0), (1, 0, 2), (0, 1, 0), (1, 1, 1), (0, 2, 2), (1, 2, 3)):
                sp.dma_start(z_dram[:, t, kind, :], zs[:, src, :]).then_inc(z_out, 16)

            def stage_pos(h, par):
                z_rows = z_dram.rearrange("(h p) t k n -> h (p t) k n", p=HP)[h]
                for kind, lo, hi in ((0, 0, ZW), (1, 0, S), (2, ZB0, ZW)):
                    zr = z_rows[:, kind, :]
                    src = bass.AP(zr.tensor, zr.offset + lo, [[1, NI]] + [list(zr.ap[0])] + [[1, hi - lo]])
                    sp.dma_start(stage_z[:, par, kind, lo:hi], src).then_inc(staged[par], 16)

            sp.wait_ge(z_out, 16 * 6)
            stage_pos(0, 0)
            stage_pos(1, 1)
            for b in range(B):
                c = slice(b * S, (b + 1) * S)
                sp.wait_ge(q_split, 2 * b + 1)
                sp.dma_start(qs_dram[:, :, 1, c], rep_ap(vh[:, b, :], [(0, 2), (1, S)])).then_inc(q_out, 16)
                sp.wait_ge(v_extended, 2 * b + 2)
                sp.dma_start(qs_dram[:, :, 0, c], rep_ap(vl[:, b, :], [(NG, 2), (1, S)])).then_inc(q_out, 16)
                sp.dma_start(qs_dram[:, :, 2, c], rep_ap(vh[:, b, NG:], [(0, 2), (1, S)])).then_inc(q_out, 16)
                sp.wait_ge(q_split, 2 * b + 2)
                for t, src in ((0, uh), (2, ul)):
                    sp.dma_start(qc_dram[:, t:t + 2, c], rep_ap(src[:, c], [(0, 2), (1, S)]))\
                        .then_inc(u_out[b], 16)
                if b < B - 1:
                    sp.wait_ge(k_split, b + 1)
                else:
                    sp.wait_ge(k_split_last, 1)
                for t in (0, 2):
                    sp.dma_start(kc_dram[:, t:t + 2, b, :], rep_ap(kh[:, c], [(B * S, 2), (1, S)]))\
                        .then_inc(k_out, 16)
            sp.wait_ge(q_out, 16 * 3 * B)
            sp.wait_ge(stage_zero, 8)
            stage_queries(sp, 0, 0, staged[0], range(NI - 2))
            sp.wait_ge(k_out, 32 * B)
            stage_keys(sp, 0, 0, staged[0])
            sp.wait_ge(ff[0]["x_new"], NT)
            sp.wait_ge(v_ready, B)
            vr = v_rep[:, :, :].rearrange("p (t k) n -> p t k n", k=4)
            for quad in range(4):
                for kq in range(4):
                    sp.dma_start(vr[32 * quad:32 * quad + 32, :, kq, :],
                                 v_sb[32 * kq:32 * kq + 32, :, :]).then_inc(v_rep_in, 16)
            for b in range(B):
                sp.wait_ge(u_out[b], 32)
                stage_content(sp, 1, 1, b, staged[1])
            stage_keys(sp, 1, 1, staged[1])
            stage_queries(sp, 1, 1, staged[1])

            def stage(h, par):
                stage_pos(h, par)
                for b in range(B):
                    stage_content(sp, h, par, b, staged[par])
                stage_keys(sp, h, par, staged[par])
                stage_queries(sp, h, par, staged[par])

            sp.wait_ge(scores_ready, NP)
            stage(2, 0)

            def send_o(h, par):
                sp.wait_ge(o_ready, h + 1)
                sp.dma_start(at_dram[h].rearrange("p j n -> j p n"),
                             o_sb[:, par, :]).then_inc(o_out[par], 16)

            with sp.Fori(0, (H - 4) // 2) as it:
                for k in range(2):
                    par = (3 + k) % 2
                    sp.wait_ge(scores_ready, (it * 2 + (2 + k)) * NP)
                    stage(it * 2 + (3 + k), par)
                    send_o(it * 2 + k, k)
            sp.wait_ge(scores_ready, (H - 2) * NP)
            stage(H - 1, 1)
            def read_o(h):
                sp.dma_start(attnT[HP * h:HP * h + HP, :], at_dram[h]).then_inc(attn_in, 16)

            for h in (H - 4, H - 3):
                send_o(h, h % 2)
            for par in range(2):
                sp.wait_ge(o_out[par], 16 * (H // 2 - 1))
            for h in range(H - 2):
                read_o(h)
            for h in (H - 2, H - 1):
                send_o(h, h % 2)
                sp.wait_ge(o_out[h % 2], 16 * (H // 2))
                read_o(h)
            ov = out.rearrange("b (t p) d -> (b t) p d", p=128)
            for t in range(NT):
                sp.wait_ge(ff[1]["x_new"], t + 1)
                sp.dma_start(ov[t], x[:, t, :]).then_inc(out_done, 16)
            sp.wait_ge(out_done, 16 * NT)

        @block.gpsimd
        def _(pool):
            nc.gpsimd.memset(ones[:, :], 1.0).then_inc(ones_set, 1)
            nc.gpsimd.memset(minus_half[:, :], -0.5).then_inc(ones_set, 1)
            nc.gpsimd.memset(mean16[:, :], 1.0 / HID).then_inc(ones_set, 1)
            nc.gpsimd.memset(w2c[:, :, D:D + 1], 1.0 / HID).then_inc(ones_set, 1)
            pool.wait_ge(ones_set, 4)
            nc.gpsimd.memset(zs[:, :, :].bitcast(U32), 0).then_inc(zs_zero, 1)
            nc.gpsimd.memset(stage_c[:, 0, :].bitcast(U32), 0).then_inc(stage_zero, 1)

            def ln_rstd(f, g, groups=1):
                s = ln[f]
                tiles = slice(4 * g, 4 * (g + groups))
                var, r = mv[:, tiles, 1], rs[:, tiles]
                pool.wait_ge(s["mean"], tiles.stop)
                m, a = (1.0, EPS) if f == 1 else (1 + EPS, EPS * EPS)
                nc.gpsimd.tensor_scalar(r, var, m, a, ALU.mult, ALU.add).then_inc(s["rstd0_"], groups)
                pool.wait_ge(s["rstd0_"], g + groups)
                nc.gpsimd.tensor_tensor(r, r, minus_half[:, 0:4 * groups], ALU.pow).then_inc(s["rstd"], groups)

            def ln_low(f, g):
                s = ln[f]
                c = slice(g * 512, (g + 1) * 512)
                pool.wait_ge(s["xT"], 2 * g + 2)
                nc.gpsimd.tensor_tensor(xT_low[:, c], xT[:, c], xT_high[:, c], ALU.subtract)\
                    .then_inc(s["xT_low"], 1)

            def zero_stage(par, n):
                if n == 3:
                    nc.gpsimd.memset(stage_c[:, par, :].bitcast(U32), 0).then_inc(stage_zero, 1)
                else:
                    nc.gpsimd.memset(stage_q[:, par, n, :].bitcast(U32), 0).then_inc(stage_zero, 1)

            def ffn(f):
                s = ff[f]
                for n in range(STEPS[f]):
                    if n in TURN_STEPS[f] and (f == 0 or n):
                        ln_low(2 * f, TURN_STEPS[f][n])
                    if n in (1, 3) and f == 0:
                        ln_rstd(2 * f, (1, 3).index(n) + 2)
                    g = (n - 2) // 4
                    if n % 4 == 2 and g < B:
                        pool.wait_ge(ln[2 * f]["xhat"], 4 * g + 4)
                        if n == 2 and f == 0:
                            pool.wait_ge(const_ready, 1)
                        part = x[:, 4 * g:4 * g + 4, :]
                        nc.gpsimd.tensor_tensor(part, part, rep_ap(half_const[:, :], [(0, 4), (1, D)]), ALU.add)\
                            .then_inc(s["x_const"], 1)
                    g = (n - 8) // 4
                    if n % 4 == 0 and 0 <= g < B:
                        r, v = grs[:, 4 * g:4 * g + 4], gvar[:, 4 * g:4 * g + 4]
                        pool.wait_ge(s["gvar"], g + 1)
                        nc.gpsimd.tensor_scalar(r, v, 0.0, EPS, ALU.max, ALU.add).then_inc(s["gvar_eps"], 1)
                        pool.wait_ge(s["gvar_eps"], g + 1)
                        nc.gpsimd.tensor_tensor(r, r, minus_half[:, 0:4], ALU.pow).then_inc(s["grstd"], 1)
                    if f == 1:
                        continue
                    if n % 4 == 1 and 0 <= (n - 9) // 4 < B:
                        ln_rstd(1, (n - 9) // 4)
                    if n == 0:
                        zero_stage(1, 0)
                        zero_stage(1, 1)
                    if n == 3:
                        zero_stage(1, 2)
                        zero_stage(1, 3)
                    if n in (5, 9):
                        nc.gpsimd.memset(v_diag[:, n // 9, :, :, :], 0.0).then_inc(v_diag_zero, 1)
                    if n - 1 in QK_STEPS:
                        b = QK_STEPS[n - 1]
                        pool.wait_ge(q_split, 2 * b + 1)
                        nc.gpsimd.tensor_copy(vl[:, b, S:VW], vl[:, b, 1:NG + 1]).then_inc(v_extended, 1)
                        nc.gpsimd.tensor_copy(vh[:, b, S:VW], vh[:, b, 1:NG + 1]).then_inc(v_extended, 1)
                        if b < B - 1:
                            c = slice(b * S, (b + 1) * S)
                            pool.wait_ge(k_high, 2 * b + 2)
                            nc.gpsimd.tensor_tensor(kl[:, c], k_full, kh[:, c], ALU.subtract).then_inc(k_split, 1)
                    if n in (22, 24, 26):
                        b = (22, 24, 26).index(n)
                        pool.wait_ge(u_out[b], 32)
                        stage_content(pool, 0, 0, b, staged_first)

            ln_rstd(0, 0)
            for n in range(3):
                zero_stage(0, n)
            ln_low(0, 0)
            ln_rstd(0, 1)
            ffn(0)
            pool.wait_ge(q_out, 16 * 3 * B)
            pool.wait_ge(stage_zero, 8)
            stage_queries(pool, 0, 0, staged_first, range(NI - 2, NI))
            pool.wait_ge(u_out[B - 1], 32)
            stage_content(pool, 0, 0, B - 1, staged_first)

            def spread_v(h, par):
                for quad in range(4):
                    q = slice(32 * quad, 32 * quad + 32)
                    pool.wait_ge(v_diag_ready, h * 4 + quad)
                    nc.gpsimd.tensor_copy(v_diag[q, par, :, quad, :],
                                          v_rep[q, :, bass.ds(h * HP, HP)]).then_inc(v_diag_ready, 1)

            pool.wait_ge(v_diag_zero, 2)
            pool.wait_ge(v_rep_in, 16 * 16)
            spread_v(1, 1)
            pool.wait_ge(v_diag_ready, 8)
            for g in range(B):
                part = x[:, 4 * g:4 * g + 4, :]
                nc.gpsimd.tensor_tensor(part, part, rep_ap(bo_row, [(0, 4), (1, D)]), ALU.add)\
                    .then_inc(x_bo, 1)
            pool.wait_ge(x_bo, B)
            with pool.Fori(0, (H - 2) // 2) as it:
                for k in range(2):
                    pool.wait_ge(av_ready, it * 2 + (k + 1))
                    spread_v(it * 2 + (2 + k), k)
            pool.wait_ge(v_diag_ready, 4 * H)
            for b in (1, 3):
                c = slice(b * S, (b + 1) * S)
                pool.wait_ge(attn_in, 16 * H)
                pool.wait_ge(rec_out, 4 * (b // 2 + 1))
                nc.gpsimd.tensor_tensor(attnT[:, c], attnT[:, c], rec_tokens[:, b // 2, :], ALU.mult)\
                    .then_inc(attn_scaled_odd, 1)
            ln_rstd(2, 0)
            ln_rstd(2, 1)
            ln_low(2, 0)
            ln_rstd(2, 2)
            ln_low(2, 1)
            ln_rstd(2, 3)
            ffn(1)

        @block.scalar
        def _(act):
            act.dma_start(pTf[:, 14336:15360], w12_d).then_inc(w_in, 16)
            act.dma_start(ident[:, :], ident_d).then_inc(ident_in, 16)
            act.dma_start(vectors[:, :], vectors_d).then_inc(vectors_in, 16)
            act.dma_start(rows[:, :, :].rearrange("p a n -> p (a n)"),
                          bass.AP(rows_d.tensor, rows_d.offset, [[0, 128], [1, 3 * D]])).then_inc(rows_in, 16)

            def ln_evac(f, g):
                s = ln[f]
                act.wait_ge(s["turned"], 4 * g + 4)
                c = slice(g * 512, (g + 1) * 512)
                src = ps[ln_bank(f, g)]
                if f == 1:
                    nc.scalar.activation(xT[:, c], src, ACT.Copy).then_inc(s["xT"], 1)
                else:
                    nc.scalar.activation(xT_high[:, c], src, ACT.Identity, scale=g1c, bias=lb1c)\
                        .then_inc(s["xT"], 1)
                    nc.scalar.activation(xT[:, c], src, ACT.Identity, scale=g1c, bias=lb1c)\
                        .then_inc(s["xT"], 1)

            def q_high_halves(b):
                if b == 0:
                    act.wait_ge(bias_cols_ready, 2)
                act.wait_ge(q_mm, b + 1)
                for n, (hi, bias) in enumerate(((vh[:, b, 0:S], qvc), (uh[:, b * S:(b + 1) * S], quc))):
                    dst, src = by_row(1 - n, hi, ps[QK_BANKS[b][0]])
                    nc.scalar.activation(dst, src, ACT.Identity, bias=bias).then_inc(q_high, 1)

            def k_high_half(b):
                act.wait_ge(k_mm, b + 1)
                nc.scalar.activation(kh[:, b * S:(b + 1) * S], ps[QK_BANKS[b][1]], ACT.Identity,
                                     bias=bkc).then_inc(k_high, 1)
                if b < B - 1:
                    if b:
                        act.wait_ge(k_split, b)
                    nc.scalar.activation(k_full, ps[QK_BANKS[b][1]], ACT.Identity, bias=bkc).then_inc(k_high, 1)

            def ffn(f):
                s = ff[f]
                for n in range(STEPS[f]):
                    g, c = divmod(n, HC)
                    if n < NT:
                        act.wait_ge(s["hid"], n + 1)
                        if g >= 2:
                            act.wait_ge(s["ffn"], 4 * (g - 1))
                        nc.scalar.activation(ge[:, n % 8, :], ps[n % 2], ACT.Gelu, scale=wstep[:, 0:1],
                                             bias=b1c[:, c:c + 1]).then_inc(s["gelu"], 1)
                    if n in TURN_STEPS[f]:
                        ln_evac(2 * f, TURN_STEPS[f][n])
                    m = n - 1
                    if 0 <= m < NT:
                        act.wait_ge(s["gelu"], m + 1)
                        if m == 0 and f == 0:
                            act.wait_ge(pivot_ready, 1)
                        if m >= 3:
                            act.wait_ge(s["sq_summed"], sums(m - 3))
                        nc.scalar.activation(sq[:, m % 3, :], ge[:, m % 8, :], ACT.Square,
                                             bias=minus_pivot).then_inc(s["squared"], 1)
                    if f == 1:
                        continue
                    if n == 5:
                        act.wait_ge(pos_mm, 1)
                        nc.scalar.activation(pf, ps[5], ACT.Identity, bias=bpc).then_inc(pos_f, 1)
                    if n in TURN1_STEPS:
                        ln_evac(1, TURN1_STEPS[n])
                    if n - 1 in QK_STEPS:
                        q_high_halves(QK_STEPS[n - 1])
                        k_high_half(QK_STEPS[n - 1])

            act.wait_ge(vectors_in, 16)
            nc.scalar.activation(gelu_b1, b1c, ACT.Gelu).then_inc(gelu_b1_ready, 1)
            ln_evac(0, 0)
            act.wait_ge(tern_turned, 1)
            nc.scalar.activation(w1T[:, :], ps[0], ACT.Copy).then_inc(w1_ready, 1)
            ffn(0)

            def exp_tile(h, q):
                if q % 2 == 0:
                    act.wait_ge(max_ready, h * NP + (q // 2 + 1))
                    if not (isinstance(h, int) and h * NQ + q < 6):
                        act.wait_ge(pT_ready, slot_before(h, q // 2))
                nc.scalar.activation(probs[:, q % 6, :], score_pair(q // 2)[:, q % 2, :], ACT.Exp,
                                     bias=negmax[:, q % 8:q % 8 + 1],
                                     accum_out=rowsum[:, bass.ds(h * NQ + q, 1)]).then_inc(probs_ready, 1)

            def take_o(h, par, pair):
                act.wait_ge(av_ready, h + 1)
                if not (isinstance(h, int) and h < 2):
                    act.wait_ge(o_out[par], pair * 16)
                nc.scalar.activation(o_sb[:, par, :], ps[4 + par][:, 0:128], ACT.Copy).then_inc(o_ready, 1)

            for h in range(2):
                for q in range(NQ):
                    exp_tile(h, q)
                    if h == 0 and 7 <= q < 11:
                        quad = q - 7
                        rows32 = slice(32 * quad, 32 * quad + 32)
                        act.wait_ge(v_diag_zero, 2)
                        act.wait_ge(v_rep_in, 16 * 16)
                        nc.scalar.activation(v_diag[rows32, 0, :, quad, :], v_rep[rows32, :, 0:HP],
                                             ACT.Copy).then_inc(v_diag_ready, 1)
            for h in range(2, 4):
                for q in range(NQ):
                    exp_tile(h, q)
                    if q == 3:
                        take_o(h - 2, h % 2, 0)
            with act.Fori(0, (H - 4) // 2) as it:
                for k in range(2):
                    for q in range(NQ):
                        exp_tile(it * 2 + (4 + k), q)
                        if q == 3:
                            take_o(it * 2 + (2 + k), k, it + 1)
            take_o(H - 2, 0, H // 2 - 1)
            nc.scalar.activation(gelu_b1, b1c, ACT.Gelu)
            take_o(H - 1, 1, H // 2 - 1)
            for b in (1, 3):
                for n in range(4):
                    act.wait_ge(rec_turned, n + 1)
                    nc.scalar.activation(
                        rec_tokens[:, b // 2, :].rearrange("p (j q i) -> p q j i", j=4, q=NQ)[:, 4 * n:4 * n + 4],
                        ps[n].rearrange("p (q j b i) -> p b q j i", q=4, j=4, b=B)[:, b],
                        ACT.Copy).then_inc(rec_out, 1)
            ln_evac(2, 0)
            ffn(1)

        @block.vector
        def _(dve):
            steps = [0]

            def chain(ins):
                ins.then_inc(dve_step, 1)
                steps[0] += 1
                dve.wait_ge(dve_step, steps[0])

            def ln_stats(f, g):
                s = ln[f]
                for t in range(4 * g, 4 * g + 4):
                    x_made(dve, f, t)
                    if t == 4 * g and (g or f):
                        dve.wait_ge(ln[f if g else f - 1]["mean"], 4 * g if g else NT)
                    nc.vector.bn_stats(stat[:, t % 4, :], x[:, t, :]).then_inc(s["stat"], 1)
                for t in range(4 * g, 4 * g + 4):
                    dve.wait_ge(s["stat"], t + 1)
                    nc.vector.bn_aggr(mv[:, t, :], stat[:, t % 4, :]).then_inc(s["mean"], 1)

            def ln_xhat(f, t):
                s = ln[f]
                dve.wait_ge(s["rstd"], t // 4 + 1)
                if t >= 4:
                    dve.wait_ge(s["turned"], t - 3)
                nc.vector.tensor_scalar(xh[:, t % 4, :], x[:, t, :], mv[:, t, 0:1], rs[:, t:t + 1],
                                        ALU.subtract, ALU.mult).then_inc(s["xhat"], 1)

            def ln_xhats(f, g):
                for t in range(4 * g, 4 * g + 4):
                    ln_xhat(f, t)

            def ternary(n, w):
                sc = wscale[:, n:n + 1]
                nc.vector.tensor_scalar(tmp_t[:, 0, :], w, sc, 0.5, ALU.mult, ALU.is_gt)
                chain(nc.vector.tensor_scalar(tmp_t[:, 1, :], w, sc, -0.5, ALU.mult, ALU.is_lt))
                nc.vector.tensor_tensor(tern[:, n, :], tmp_t[:, 0, :], tmp_t[:, 1, :], ALU.subtract)\
                    .then_inc(tern_ready, 1)
                dve.wait_ge(tern_ready, n + 1)

            ln_stats(0, 0)
            dve.wait_ge(w_in, 16)
            nc.vector.tensor_reduce(wsum[:, 0:1], w1_sb, AX.XY, ALU.add,
                                    apply_absolute_value=True)
            nc.vector.tensor_reduce(wsum[:, 1:2], w2_sb, AX.X, ALU.add,
                                    apply_absolute_value=True).then_inc(wsum_ready, 1)
            ln_xhats(0, 0)
            dve.wait_ge(wtotal_ready, 1)
            chain(nc.vector.tensor_scalar(wclip, ps[2][:, 0:2], 1.0 / (D * HID), 1e-5, ALU.mult, ALU.max))
            chain(nc.vector.reciprocal(wscale, wclip))
            nc.vector.reciprocal(wstep, wscale).then_inc(step_ready, 1)
            ternary(0, w1_sb.rearrange("p c n -> p (c n)"))
            ln_stats(0, 1)
            ternary(1, w2_sb)
            dve.wait_ge(step_ready, 1)
            nc.vector.tensor_scalar(half_step, wstep[:, 1:2], 0.5, None, ALU.mult).then_inc(half_step_ready, 1)
            ln_xhats(0, 1)
            dve.wait_ge(pivot_summed, 1)
            chain(nc.vector.tensor_reduce(pivot_sum, ps[5][:, 0:HC], AX.X, ALU.add, negate=True))
            nc.vector.tensor_scalar(minus_pivot, pivot_sum, 1.0 / HID, None, ALU.mult).then_inc(pivot_ready, 1)
            dve.wait_ge(vectors_in, 16)
            dve.wait_ge(tern_turned, 2)
            dve.wait_ge(half_step_ready, 1)
            for dst, v, done in ((w2g, g2c, w2g_ready), (w2b, lb2c, w2b_ready)):
                nc.vector.scalar_tensor_tensor(dst, ps[3].rearrange("p (c n) -> p c n", c=HC), half_step,
                                               rep_ap(v, [(1, HC), (0, D)]), ALU.mult, ALU.mult)\
                    .then_inc(done, 1)
            ln_stats(0, 2)
            def centre_w2():
                dve.wait_ge(w2g_ready, 1)
                dve.wait_ge(w2_summed, 1)
                nc.vector.scalar_tensor_tensor(w2c[:, :, 0:D], rep_ap(ps[4][:, 0:D], [(0, HC), (1, D)]),
                                               -1.0 / HID, w2g, ALU.mult, ALU.add).then_inc(w2_ready, 1)
                dve.wait_ge(rows_in, 16)
                dve.wait_ge(const_summed, 1)
                nc.vector.scalar_tensor_tensor(half_const[:, :], b2_row, 0.5, ps[2][:, 0:D],
                                               ALU.mult, ALU.add).then_inc(const_ready, 1)

            def split_positions():
                dve.wait_ge(pos_f, 1)
                dve.wait_ge(zs_zero, 1)
                chain(nc.vector.tensor_copy(zs[:, 0, 0:S], pf))
                nc.vector.tensor_copy(zs[:, 2, S + 1:2 * S], zs[:, 0, 0:S - 1]).then_inc(pos_split, 1)
                chain(nc.vector.tensor_tensor(zs[:, 1, 0:S], pf, zs[:, 0, 0:S], ALU.subtract))
                nc.vector.tensor_copy(zs[:, 3, S + 1:2 * S], zs[:, 1, 0:S - 1]).then_inc(pos_split, 1)

            def query_biases():
                for dst, src in ((quc, uc), (qvc, vc)):
                    chain(nc.vector.tensor_tensor(dst, bqc, src, ALU.add))
                    nc.vector.tensor_scalar(dst, dst, SCALE, None, ALU.mult).then_inc(bias_cols_ready, 1)
                dve.wait_ge(qkv_weights_in, 16)
                nc.vector.tensor_scalar(wq_s, wq_sb, SCALE, None, ALU.mult).then_inc(wq_scaled, 1)

            def add_attention(b):
                dve.wait_ge(wo_mm, b + 1)
                dve.wait_ge(x_bo, B)
                nc.vector.tensor_tensor(x[:, 4 * b:4 * b + 4, :], x[:, 4 * b:4 * b + 4, :],
                                        ps[4 + b % 2].rearrange("p (t n) -> p t n", t=4), ALU.add)\
                    .then_inc(x_attn, 1)

            def ffn(f):
                s = ff[f]
                for n in range(STEPS[f]):
                    g = (n - 8) // 4
                    if n % 4 == 0 and 0 <= g < B:
                        cols4 = slice(4 * g, 4 * g + 4)
                        dve.wait_ge(s["ffn"], 4 * g + 4)
                        dve.wait_ge(s["sq_mean"], g + 1)
                        mean = moments(g)[:, :, 0:2 * (D + 1)].rearrange("p a (t n) -> p a t n", t=2)[:, :, :, D]
                        nc.vector.tensor_scalar(gmean[:, cols4].rearrange("p (a t) -> p a t", a=2), mean,
                                                minus_pivot, None, ALU.add).then_inc(s["gmean"], 1)
                        dve.wait_ge(s["gmean"], g + 1)
                        nc.vector.tensor_tensor(gmean[:, cols4], gmean[:, cols4], gmean[:, cols4], ALU.mult)\
                            .then_inc(s["gmean_sq"], 1)
                        dve.wait_ge(s["gmean_sq"], g + 1)
                        nc.vector.tensor_tensor(gvar[:, cols4], moments(g)[:, 0, SQ0:SQ0 + 4], gmean[:, cols4],
                                                ALU.subtract).then_inc(s["gvar"], 1)
                    m = n - 1
                    g, c = divmod(m, HC)
                    if 0 <= m < NT and c:
                        dve.wait_ge(s["squared"], m + 1)
                        if m > 1:
                            dve.wait_ge(s["sq_summed"], sums(m) - 1)
                        if c == 1 and g:
                            dve.wait_ge(s["sq_split"], 2 * g)
                        first = sq[:, (m - 1) % 3, :] if c == 1 else sqsum[:, :]
                        nc.vector.tensor_tensor(sqsum[:, :], first, sq[:, m % 3, :],
                                                ALU.add).then_inc(s["sq_summed"], 1)
                    if 0 <= m < NT and c == HC - 1:
                        dve.wait_ge(s["sq_summed"], sums(m))
                        if g:
                            dve.wait_ge(s["sq_mean"], g)
                        nc.vector.tensor_copy(sq_high, sqsum[:, :]).then_inc(s["sq_split"], 1)
                        dve.wait_ge(s["sq_split"], 2 * g + 1)
                        nc.vector.tensor_tensor(sq_low, sqsum[:, :], sq_high, ALU.subtract).then_inc(s["sq_split"], 1)
                    g = (n - 9) // 4
                    if n % 4 == 1 and 0 <= g < B:
                        dve.wait_ge(s["grstd"], g + 1)
                        dve.wait_ge(s["x_const"], g + 1)
                        for t in range(4 * g, 4 * g + 4):
                            nc.vector.scalar_tensor_tensor(x[:, t, :], out_tile(t)[:, 0:D], grs[:, t:t + 1],
                                                           x[:, t, :], ALU.mult, ALU.add).then_inc(s["x_new"], 1)
                    if f == 1:
                        continue
                    if n in (3, 5):
                        ln_xhats(0, (n + 1) // 2)
                    if n == 3:
                        ln_stats(0, 3)
                    if n == 6:
                        split_positions()
                    if n == 7:
                        query_biases()
                    if n % 4 == 1 and 0 <= (n - 9) // 4 < B:
                        ln_stats(1, (n - 9) // 4)
                    if n in XHAT1_STEPS:
                        ln_xhats(1, XHAT1_STEPS[n])
                    if n - 1 in QK_STEPS:
                        q_low_halves(QK_STEPS[n - 1])
                        if QK_STEPS[n - 1] == B - 1:
                            k_low_half(B - 1)
                    if n - 2 in QK_STEPS:
                        v_bias(QK_STEPS[n - 2])

            def q_low_halves(b):
                c = slice(b * S, (b + 1) * S)
                dve.wait_ge(q_high, 2 * b + 2)
                for n, (hi, lo, bias) in enumerate(((vh[:, b, 0:S], vl[:, b, 0:S], qvc), (uh[:, c], ul[:, c], quc))):
                    dst, src = by_row(1 - n, lo, ps[QK_BANKS[b][0]])
                    high = by_row(1 - n, hi, ps[QK_BANKS[b][0]])[0]
                    for j in range(4 if n else 1):
                        part = (slice(None), j) if n else (slice(None),)
                        ins = nc.vector.scalar_tensor_tensor(dst[part], src[part], bias, high[part],
                                                             ALU.add, ALU.subtract)
                    ins.then_inc(q_split, 1)

            def k_low_half(b):
                c = slice(b * S, (b + 1) * S)
                dve.wait_ge(k_high, 2 * b + 1)
                nc.vector.scalar_tensor_tensor(kl[:, c], ps[QK_BANKS[b][1]], bkc, kh[:, c], ALU.add, ALU.subtract)\
                    .then_inc(k_split_last, 1)

            def v_bias(b):
                dve.wait_ge(v_mm, b + 1)
                nc.vector.tensor_tensor(v_sb[:, 4 * b:4 * b + 4, :], ps[2].rearrange("p (t n) -> p t n", t=4),
                                        rep_ap(bv_row, [(0, 4), (1, D)]), ALU.add).then_inc(v_ready, 1)

            centre_w2()
            ffn(0)
            for b in range(B):
                dve.wait_ge(u_out[b], 32)
            dve.wait_ge(k_out, 32 * B)
            dve.wait_ge(q_out, 16 * 3 * B)

            def row_max(h, n):
                dve.wait_ge(scores_ready, h * NP + (n + 1))
                nc.vector.tensor_reduce(negmax[:, 2 * n % 8:2 * n % 8 + 2], score_pair(n)[:, :, :], AX.X,
                                        ALU.max, negate=True).then_inc(max_ready, 1)

            def turn(h, par, n):
                dve.wait_ge(probs_ready, h * NQ + (2 * n + 2))
                if n == 0 and isinstance(h, int) and h == 1:
                    dve.wait_ge(v_rep_in, 16 * 16)
                if n == 0 and not (isinstance(h, int) and h < 2):
                    dve.wait_ge(av_ready, h - 1)
                nc.vector.transpose(pT[:, par, 2 * n:2 * n + 2, :].rearrange("p a s -> p (a s)"),
                                    probs[:, 2 * n % 6:2 * n % 6 + 2, :].rearrange("p a s -> p (a s)"))\
                    .then_inc(pT_ready, 1)

            def head(h, par, first=False):
                for n in range(NP):
                    row_max(h, n)
                    if n >= 1:
                        turn(h, par, n - 1)
                    elif not first:
                        turn(h - 1, 1 - par, NP - 1)

            head(0, 0, True)
            head(1, 1)
            head(2, 0)
            head(3, 1)
            with dve.Fori(0, (H - 4) // 2) as it:
                for k in range(2):
                    head(it * 2 + (4 + k), k)
            turn(H - 1, 1, NP - 1)

            dve.wait_ge(av_ready, H - 1)
            nc.vector.reciprocal(rec, rowsum[:, :]).then_inc(rec_ready, 1)
            dve.wait_ge(rec_ready, 1)
            src = rec.rearrange("p (h q) -> p q h", q=NQ)
            for e in range(HP):
                ins = nc.vector.tensor_copy(recx[:, :, :, e], src)
            ins.then_inc(recx_ready, 1)
            dve.wait_ge(attn_in, 16 * H)
            av = attnT.rearrange("p (b j q i) -> p b q j i", b=B, j=4, q=NQ)

            def scale_attention(b):
                for n in range(4):
                    dve.wait_ge(rec_turned, n + 1)
                    r = ps[n].rearrange("p (q j b i) -> p b q j i", q=4, j=4, b=B)[:, b]
                    a = av[:, b, 4 * n:4 * n + 4]
                    ins = nc.vector.tensor_tensor(a, a, r, ALU.mult)
                ins.then_inc(attn_scaled, 1)

            dve.wait_ge(rec_out, 8)
            scale_attention(0)
            scale_attention(2)
            for b in range(B):
                add_attention(b)
                ln_stats(2, b)
                if b:
                    ln_xhats(2, b - 1)
            ln_xhats(2, B - 1)
            ffn(1)

        @block.tensor
        def _(pe):
            mm = nc.tensor.matmul
            pe.wait_ge(ones_set, 1)
            pe.wait_ge(wsum_ready, 1)
            mm(ps[2][:, 0:2], ones[:, :], wsum, start=True, stop=True).then_inc(wtotal_ready, 1)

            def turn_weights(n, bank):
                pe.wait_ge(tern_ready, n + 1)
                for c in range(HC):
                    ins = nc.tensor.transpose(bank[:, c * 128:(c + 1) * 128],
                                              tern[:, n, c * 128:(c + 1) * 128], ident[:, :])
                ins.then_inc(tern_turned, 1)

            def ln_turn(f, t):
                s = ln[f]
                g = t // 4
                pe.wait_ge(s["xhat"], t + 1)
                if g >= 2:
                    pe.wait_ge(s["xT"], (g - 1) * (1 if f == 1 else 2))
                elif f == 1:
                    pe.wait_ge(ln[0]["xT"], 2 * B)
                nc.tensor.transpose(ps[ln_bank(f, g)][:, (t % 4) * 128:(t % 4 + 1) * 128], xh[:, t % 4, :],
                                    ident[:, :]).then_inc(s["turned"], 1)

            def mean_squares(s, g):
                pe.wait_ge(s["sq_split"], 2 * g + 2)
                for t in range(4):
                    k = slice(t * 128, (t + 1) * 128)
                    o = moments(g)[:, 0, SQ0 + t:SQ0 + t + 1]
                    mm(o, sq_high[:, k], mean16[:, :], start=True, stop=False)
                    ins = mm(o, sq_low[:, k], mean16[:, :], start=False, stop=True)
                ins.then_inc(s["sq_mean"], 1)

            def ffn(f):
                s = ff[f]
                for n in range(STEPS[f]):
                    g, c = divmod(n, HC)
                    if n < NT:
                        pe.wait_ge(ln[2 * f]["xT_low"], g + 1)
                        if n >= 2:
                            pe.wait_ge(s["gelu"], n - 1)
                        k = slice(c * 128, (c + 1) * 128)
                        tokens = slice(g * 512, (g + 1) * 512)
                        mm(ps[n % 2], w1T[:, k], xT_high[:, tokens], start=True, stop=False)
                        mm(ps[n % 2], w1T[:, k], xT_low[:, tokens], start=False, stop=True).then_inc(s["hid"], 1)
                    if n % 4 == 3 and 7 <= n < 4 * B + 3:
                        mean_squares(s, (n - 7) // 4)
                    t = n - 5
                    if 0 <= t < NT:
                        g = t // 4
                        if t == 0 and f == 0:
                            pe.wait_ge(w2_ready, 1)
                            pe.wait_ge(const_ready, 1)
                        if t == 4:
                            if f == 0:
                                pe.wait_ge(pos_f, 1)
                            else:
                                pe.wait_ge(x_attn, B)
                        if t % 4 == 0:
                            pe.wait_ge(s["gelu"], t + 4)
                            if g >= 2:
                                pe.wait_ge(s["x_new"], 4 * (g - 1))
                        k = slice(t % 4 * 128, (t % 4 + 1) * 128)
                        for c in range(HC):
                            ins = mm(out_tile(t), ge[:, (4 * g + c) % 8, k], w2c[:, c, :],
                                     start=(c == 0), stop=(c == HC - 1))
                        ins.then_inc(s["ffn"], 1)
                    if n == 4 * B + 4:
                        mean_squares(s, B - 1)
                    if n == 1 and f == 0:
                        turn_weights(1, ps[3])
                    if n in TURN_STEPS[f] and (f == 0 or n):
                        for t in range(4):
                            ln_turn(2 * f, 4 * TURN_STEPS[f][n] + t)
                    if f == 1:
                        continue
                    if n == 3:
                        pe.wait_ge(pos_weights_in, 16)
                        pe.wait_ge(pivot_ready, 1)
                        mm(ps[5], wp_sb, embT, start=True, stop=True).then_inc(pos_mm, 1)
                    if n == 2:
                        for bank, src, ready, done in ((4, w2g, w2g_ready, w2_summed),
                                                       (2, w2b, w2b_ready, const_summed)):
                            pe.wait_ge(ready, 1)
                            for c in range(HC):
                                ins = mm(ps[bank][:, 0:D], ones[:, :], src[:, c, :], start=(c == 0),
                                         stop=(c == HC - 1))
                            ins.then_inc(done, 1)
                    if n in TURN1_STEPS:
                        for t in range(4):
                            ln_turn(1, 4 * TURN1_STEPS[n] + t)
                    if n in QK_STEPS:
                        q_product(QK_STEPS[n])
                        k_product(QK_STEPS[n])
                    if n - 1 in QK_STEPS:
                        v_product(QK_STEPS[n - 1])

            def q_product(b):
                pe.wait_ge(ln[1]["xT"], b + 1)
                if b == 0:
                    pe.wait_ge(wq_scaled, 1)
                    pe.wait_ge(qkv_weights_in, 16)
                    pe.wait_ge(ff[0]["gelu"], NT)
                elif b == 2:
                    pe.wait_ge(ff[0]["x_new"], NT)
                else:
                    pe.wait_ge(q_split, 2 * ((b + 1) // 2))
                mm(ps[QK_BANKS[b][0]], wq_s, xT[:, b * S:(b + 1) * S], start=True, stop=True).then_inc(q_mm, 1)

            def k_product(b):
                if b % 2:
                    pe.wait_ge(k_split, (b + 1) // 2)
                mm(ps[QK_BANKS[b][1]], wk_sb, xT[:, b * S:(b + 1) * S], start=True, stop=True).then_inc(k_mm, 1)

            def v_product(b):
                if b:
                    pe.wait_ge(v_ready, b)
                else:
                    pe.wait_ge(ff[0]["x_new"], 3 * 4)
                for t in range(4):
                    c = slice(b * S + t * 128, b * S + (t + 1) * 128)
                    ins = mm(ps[2][:, t * 128:(t + 1) * 128], xT[:, c], wv_sb, start=True, stop=True)
                ins.then_inc(v_mm, 1)

            pe.wait_ge(ident_in, 16)
            for t in range(4):
                ln_turn(0, t)
            turn_weights(0, ps[0])
            pe.wait_ge(gelu_b1_ready, 1)
            mm(ps[5][:, 0:HC], ones[:, :], gelu_b1, start=True, stop=True).then_inc(pivot_summed, 1)
            pe.wait_ge(w1_ready, 1)
            ffn(0)
            pe.wait_ge(v_ready, B)

            def scores(h, par, q):
                if not (isinstance(h, int) and h * NQ + q < 6):
                    pe.wait_ge(probs_ready, slot_before(h, q // 2) * 2 + (q % 2 - 1))
                bank = score_pair(q // 2)[:, q % 2, :]

                def rows(a, j):
                    return a.rearrange("k (b g) -> k b g", g=NG)[:, :, j * NQ + q]

                all_rows = stage_c[:, par, :].rearrange("k (m g) -> k m g", g=NQ)[:, :, q]
                mm(bank, all_rows, stage_k[:, par, :], start=True, stop=False, skip_group_check=True)
                for j in range(4):
                    a0 = 128 * j + NI * q
                    o = bank[32 * j:32 * j + 32, :]
                    m0 = S - NI - a0
                    mm(o, rows(stage_q[:, par, 0, :], j), stage_z[:, par, 0, m0:m0 + S], start=False,
                       stop=False, skip_group_check=True)
                for j in range(4):
                    a0 = 128 * j + NI * q
                    n = a0 + NI
                    m0 = S - NI - a0
                    mm(bank[32 * j:32 * j + 32, 0:n], rows(stage_q[:, par, 1, :], j),
                       stage_z[:, par, 1, m0:m0 + n], start=False, stop=False, skip_group_check=True)
                for j in range(4):
                    a0 = 128 * j + NI * q
                    m0 = S - NI - a0
                    ins = mm(bank[32 * j:32 * j + 32, a0 + 2:S], rows(stage_q[:, par, 2, :], j),
                             stage_z[:, par, 2, m0 + a0 + 2:m0 + S], start=False, stop=True,
                             skip_group_check=True)
                if q % 2:
                    ins.then_inc(scores_ready, 1)

            def values(h, par, kb, q0=0, q1=NQ):
                if kb == 0:
                    pe.wait_ge(pT_ready, h * NP + q1 // 2)
                    pe.wait_ge(v_diag_ready, (h + 1) * 4)
                    if not (isinstance(h, int) and h < 2):
                        pe.wait_ge(o_ready, h - 1)
                for b in range(B):
                    mov = pT[:, par, q0:q1, 32 * kb + NI * b:32 * kb + NI * (b + 1)]
                    ins = mm(ps[4 + par][32 * b:32 * b + 32, NI * q0:NI * q1],
                             v_diag[:, par, b * KB + kb, :, :].rearrange("p j e -> p (j e)"), mov,
                             start=(kb == 0), stop=(kb == KB - 1), skip_group_check=True)
                if kb == KB - 1 and q1 == NQ:
                    ins.then_inc(av_ready, 1)

            LAG = 6

            def head(h, par, staged_count, first=False):
                pe.wait_ge(staged[par], staged_count)
                for q in range(NQ):
                    scores(h, par, q)
                    if not first and q >= LAG:
                        values(h - 1, 1 - par, q - LAG)
                if not first:
                    for kb in range(NQ - LAG, KB):
                        values(h - 1, 1 - par, kb)

            pe.wait_ge(staged_first, 16 * LOADS_FIRST)
            head(0, 0, 16 * (LOADS - LOADS_FIRST), True)
            head(1, 1, 16 * LOADS)
            head(2, 0, 16 * (2 * LOADS - LOADS_FIRST))
            with pe.Fori(0, (H - 4) // 2) as it:
                for k in range(2):
                    head(it * 2 + (3 + k), 1 - k, (it + (2 + k)) * (16 * LOADS) - 16 * LOADS_FIRST * k)
            head(H - 1, 1, (H // 2) * 16 * LOADS)
            for kb in range(KB):
                values(H - 1, 1, kb, 0, NQ // 2)
            for kb in range(KB):
                values(H - 1, 1, kb, NQ // 2, NQ)
            pe.wait_ge(recx_ready, 1)
            for n in range(4):
                for q in range(4 * n, 4 * n + 4):
                    ins = mm(ps[n][:, (q % 4) * 128:(q % 4 + 1) * 128],
                             recx[:, q, :, :].rearrange("p h e -> p (h e)"), ident[:, :], start=True, stop=True)
                ins.then_inc(rec_turned, 1)
            pe.wait_ge(o_ready, H)
            pe.wait_ge(wo_in, 16)
            for b in range(B):
                pe.wait_ge((attn_scaled, attn_scaled_odd)[b % 2], b // 2 + 1)
                if b >= 2:
                    pe.wait_ge(x_attn, b - 1)
                for t in range(4):
                    ins = mm(ps[4 + b % 2][:, t * 128:(t + 1) * 128],
                             attnT[:, b * S + t * 128:b * S + (t + 1) * 128], wo_sb[:, :],
                             start=True, stop=True)
                ins.then_inc(wo_mm, 1)
                if b == 2:
                    for t in range(4):
                        ln_turn(2, t)
            for t in range(4):
                ln_turn(2, 4 + t)
            ffn(1)


def kernel(**inputs):
    import concourse.bacc as bacc
    from concourse.bass_utils import run_bass_kernel_spmd

    pos = np.arange(S, dtype=np.float32)
    idx = np.arange(D // 2, dtype=np.float32)
    inv_freq = (np.float32(1.0) / np.float32(10000.0) ** (np.float32(2.0) * idx / np.float32(D))).astype(np.float32)
    ang = pos[:, None] * inv_freq[None, :]
    emb = np.concatenate([np.sin(ang), np.cos(ang)], axis=-1).astype(np.float32)

    nc = bacc.Bacc("TRN2", target_bir_lowering=False, num_devices=1)
    a = {n: np.asarray(v) for n, v in inputs.items()}
    at = {n[3:]: v for n, v in a.items()}
    vectors = [at[n].reshape(-1) for n in ("ffn_ln1_g", "ffn_ln1_b", "attn_bq", "attn_u", "attn_v", "attn_bk",
                                           "attn_bp", "ffn_ln2_g", "ffn_ln2_b", "ffn_b1")]
    laid_out = [
        ("x", at["attn_x"]),
        ("w12", np.concatenate([at["ffn_w1"].reshape(HC, 128, D).transpose(1, 0, 2).reshape(128, HID),
                                at["ffn_w2"]], axis=1)),
        ("vectors", np.concatenate(vectors).reshape(-1, 128).T),
        ("rows", np.concatenate([at["ffn_b2"], at["attn_bo"], at["attn_bv"]])),
        ("wqkv", np.concatenate([at["attn_Wq"], at["attn_Wk"], at["attn_Wv"]], axis=1)),
        ("wo", at["attn_Wo"]),
        ("wp_emb", np.concatenate([at["attn_Wp"], emb.T], axis=1)),
        ("ident", np.eye(128, dtype=np.float32)),
    ]
    arrays, args = {}, []
    for name, value in laid_out:
        value = np.ascontiguousarray(value)
        arrays[f"in_{name}"] = value
        args.append(nc.dram_tensor(f"in_{name}", value.shape, mybir.dt.from_np(value.dtype),
                                   kind="ExternalInput").ap())
    out = nc.dram_tensor("out_0", (B, S, D), F32, kind="ExternalOutput").ap()
    macaron_kernel(nc, args, out)
    r = run_bass_kernel_spmd(nc, [arrays], core_ids=[0])
    return r.results[0]["out_0"]
```
